# Optimizing a Trainium2 kernel written in Bass

```python
import numpy as np
import jax
import jax.numpy as jnp

def _softmax(x, axis=-1):
    return jax.nn.softmax(x, axis=axis)
def _gelu(x):
    return jax.nn.gelu(x, approximate=True)
def _silu(x):
    return jax.nn.silu(x)
def _sigmoid(x):
    return jax.nn.sigmoid(x)
def _layernorm(x, axis=-1, eps=1e-5):
    m = jnp.mean(x, axis=axis, keepdims=True)
    v = jnp.var(x, axis=axis, keepdims=True)
    return (x - m) / jnp.sqrt(v + eps)
def _scatter_add(tgt, idx, src, axis=0):
    return tgt.at[idx].add(src)
def _segment_sum(src, seg, n):
    return jax.ops.segment_sum(src, seg, n)

kernel_name = 'mk_metaformer_d1_conv_nhwc128_0a876b'

def setup_inputs(seed: int = 0):
    np.random.seed(seed)
    _w = jnp.asarray
    def _rec_inputs():
        import jax
        import jax.numpy as jnp
        _gk = jax.random.key(seed)
        x = -0.0003929 + 0.9999 * jax.random.normal(jax.random.fold_in(_gk, 1), (32, 64, 64, 128), jnp.float32)
        return x
    x = _rec_inputs()
    def _L0_conv_setup():
        import jax, jax.numpy as jnp
        import numpy as np
        HEADS = 4
        DIM_HEAD = 32
        DIM = HEADS * DIM_HEAD
        B, H, W, C = (32, 64, 64, 128)
        LN_EPS = 1e-05
        key = jax.random.key(seed)
        k0, k1, k2, k3, k4 = jax.random.split(key, 5)
        x = jax.random.normal(k0, (B, H, W, C), dtype=jnp.float32)
        w_qkv = jax.random.normal(k1, (C, DIM * 3), dtype=jnp.float32) * (1.0 / np.sqrt(C))
        w_out = jax.random.normal(k2, (DIM, C), dtype=jnp.float32) * (1.0 / np.sqrt(DIM))
        b_out = jax.random.normal(k3, (C,), dtype=jnp.float32) * 0.01
        ln_scale = jnp.ones((C,), dtype=jnp.float32)
        return {'x': x, 'w_qkv': w_qkv, 'w_out': w_out, 'b_out': b_out, 'ln_scale': ln_scale}
    _L0_conv_all = _L0_conv_setup()
    _L0_conv_in = {k: v for k, v in _L0_conv_all.items() if k in ('w_qkv', 'w_out', 'b_out', 'ln_scale', )}
    del _L0_conv_all

    def _L0_ffn_setup():
        import jax, jax.numpy as jnp
        import numpy as np
        B, N, D, C, E, K = (8, 8192, 128, 128, 8, 2)
        key = jax.random.key(seed)
        k0, k1, k2 = jax.random.split(key, 3)
        x = jax.random.normal(k0, (B, N, D), dtype=jnp.float32)
        router_w = jax.random.normal(k1, (D, E), dtype=jnp.float32) * 0.05
        router_b = jnp.zeros((E,), dtype=jnp.float32)
        expert_w = jax.random.normal(k2, (E, D, C), dtype=jnp.float32) * (1.0 / np.sqrt(D))
        expert_b = jnp.zeros((E, C), dtype=jnp.float32)
        return {'x': x, 'router_w': router_w, 'router_b': router_b, 'expert_w': expert_w, 'expert_b': expert_b}
    _L0_ffn_all = _L0_ffn_setup()
    _L0_ffn_in = {k: v for k, v in _L0_ffn_all.items() if k in ('router_w', 'router_b', 'expert_w', 'expert_b', )}
    del _L0_ffn_all

    return {
        "x": x,
        "L0_conv_w_qkv": _L0_conv_in["w_qkv"],
        "L0_conv_w_out": _L0_conv_in["w_out"],
        "L0_conv_b_out": _L0_conv_in["b_out"],
        "L0_conv_ln_scale": _L0_conv_in["ln_scale"],
        "L0_ffn_router_w": _L0_ffn_in["router_w"],
        "L0_ffn_router_b": _L0_ffn_in["router_b"],
        "L0_ffn_expert_w": _L0_ffn_in["expert_w"],
        "L0_ffn_expert_b": _L0_ffn_in["expert_b"],
    }

def reference(x, L0_conv_w_qkv, L0_conv_w_out, L0_conv_b_out, L0_conv_ln_scale, L0_ffn_router_w, L0_ffn_router_b, L0_ffn_expert_w, L0_ffn_expert_b):
    import jax
    import jax.numpy as jnp
    def _L0_conv_ref(x, w_qkv, w_out, b_out, ln_scale):
        import jax, jax.numpy as jnp
        import numpy as np
        HEADS = 4
        DIM_HEAD = 32
        DIM = HEADS * DIM_HEAD
        B, H, W, C = (32, 64, 64, 128)
        LN_EPS = 1e-05
        b, h, w, c = x.shape
        n = h * w
        qkv = jnp.einsum('bhwc,cf->bhwf', x, w_qkv)
        q, k, v = jnp.split(qkv, 3, axis=-1)
        q = q.reshape(b, n, HEADS, DIM_HEAD)
        k = k.reshape(b, n, HEADS, DIM_HEAD)
        v = v.reshape(b, n, HEADS, DIM_HEAD)
        q = jax.nn.softmax(q, axis=-1) * (1.0 / np.sqrt(DIM_HEAD))
        k = jax.nn.softmax(k, axis=1)
        v = v * (1.0 / n)
        context = jnp.einsum('bnhd,bnhe->bhde', k, v)
        out = jnp.einsum('bhde,bnhd->bnhe', context, q)
        out = out.reshape(b, h, w, DIM)
        out = jnp.einsum('bhwd,dc->bhwc', out, w_out) + b_out
        mu = jnp.mean(out, axis=-1, keepdims=True)
        var = jnp.mean(jnp.square(out - mu), axis=-1, keepdims=True)
        out = (out - mu) * jax.lax.rsqrt(var + LN_EPS) * ln_scale
        return out

    def _L0_ffn_ref(x, router_w, router_b, expert_w, expert_b):
        import jax, jax.numpy as jnp
        import numpy as np
        B, N, D, C, E, K = (8, 8192, 128, 128, 8, 2)
        router_probs = jax.nn.softmax(x @ router_w + router_b, axis=-1)
        top_p, top_i = jax.lax.top_k(router_probs, K)
        top_p = top_p / jnp.sum(top_p, axis=-1, keepdims=True)
        expert_out = jnp.einsum('bnd,edc->bnec', x, expert_w) + expert_b
        gathered = jnp.take_along_axis(expert_out, top_i[..., None], axis=2)
        return jnp.einsum('bnk,bnkc->bnc', top_p, gathered)

    def _gn(v, G=32, eps=1e-5):
        B_, H_, W_, C_ = v.shape
        g = v.reshape(B_, H_, W_, G, C_ // G)
        m = jnp.mean(g, axis=(1, 2, 4), keepdims=True)
        s = jnp.var(g, axis=(1, 2, 4), keepdims=True)
        return ((g - m) / jnp.sqrt(s + eps)).reshape(v.shape)

    def _ln_c(v, eps=1e-6):
        m = jnp.mean(v, axis=-1, keepdims=True)
        s = jnp.var(v, axis=-1, keepdims=True)
        return (v - m) / jnp.sqrt(s + eps)

    def _ln_t(v, eps=1e-5):
        m = jnp.mean(v, axis=-1, keepdims=True)
        s = jnp.var(v, axis=-1, keepdims=True)
        return (v - m) / jnp.sqrt(s + eps)

    def _to_tokens(v):
        B_, H_, W_, C_ = v.shape
        return v.reshape(B_, H_ * W_, C_)
    def _from_tokens(t, like):
        return t.reshape(like.shape)

    x = x + _L0_conv_ref(_ln_c(x), L0_conv_w_qkv, L0_conv_w_out, L0_conv_b_out, L0_conv_ln_scale)
    t = _to_tokens(x)
    t = t + _L0_ffn_ref(_ln_t(t), L0_ffn_router_w, L0_ffn_router_b, L0_ffn_expert_w, L0_ffn_expert_b)
    x = _from_tokens(t, x)
    return x


_drawn_inputs = setup_inputs


def setup_inputs(seed=0):
    import zlib

    import numpy as np

    out = dict(_drawn_inputs(seed))
    spreads = {'L0_conv_ln_scale': (1.0, 0.2),
     'L0_ffn_router_b': (0.0, 0.1),
     'L0_ffn_expert_b': (0.0, 0.1)}
    factors = {'L0_conv_w_qkv': 8.0, 'L0_conv_w_out': 8.0}
    for name, (base, spread) in spreads.items():
        noise = np.random.default_rng([zlib.crc32(name.encode()), seed]).standard_normal(out[name].shape)
        drawn = base * np.exp(spread * noise) if base else spread * noise
        out[name] = jnp.asarray(drawn.astype(out[name].dtype))
    for name, factor in factors.items():
        out[name] = (out[name] * factor).astype(out[name].dtype)
    return out
```

```python
from contextlib import ExitStack

import concourse.bass as bass
from concourse import mybir

F32, F16, U32, I32 = mybir.dt.float32, mybir.dt.float16, mybir.dt.uint32, mybir.dt.int32
ALU = mybir.AluOpType
ACT = mybir.ActivationFunctionType
AX_X = mybir.AxisListType.X
R_MAX = bass.bass_isa.ReduceOp.max

P = 128
HEADS, DH = 4, 32
E = 8
T = 4
G = 8
TAIL = 2
W3 = 3 * P
KV = 2 * P + 4
HALF = E // 2
XS = 256.0
WS = 1024.0
LN_XS = 5.545177444479562


def at_least(eng, sem, value):
    if isinstance(value, int) and value < 1:
        return
    eng.wait_ge(sem, value)


def step_on(eng, going):
    eng.sem_inc(going, 1)


def metaformer_kernel(nc, x, w_qkv, w_out, b_out, ln_scale, router_w, router_b, expert_w, expert_b, out):
    B = x.shape[0]
    N = x.shape[1] * x.shape[2]
    assert N == G * T * P
    x_v = x.rearrange("b h w c -> b (h w) c").rearrange("b (g p t) c -> b g p (t c)", g=G, p=P)
    out_v = out.rearrange("b h w c -> b (h w) c").rearrange("b (g p t) c -> b g p (t c)", g=G, p=P)

    ctx = ExitStack()
    with ctx:
        def sb(name, shape, dt=F32):
            return ctx.enter_context(nc.sbuf_tensor(name, shape, dt))

        def ps(name, shape):
            return ctx.enter_context(nc.psum_tensor(name, shape, F32))

        def sem(name):
            return ctx.enter_context(nc.semaphore(name))

        ident = sb("ident", [P, P])
        ones = sb("ones", [P, P])
        zero_col, one_col = sb("zero_col", [P, 1]), sb("one_col", [P, 1])
        eps_ln1, eps_ln2, ln_xs = sb("eps_ln1", [P, 1]), sb("eps_ln2", [P, 1]), sb("ln_xs", [P, 1])
        expert_no = sb("expert_no", [P, T, E])
        expert_no_i = sb("expert_no_i", [P, T, E], I32)
        head_mask = sb("head_mask", [P, P])
        wq = sb("wq", [P, W3]); wq_h = sb("wq_h", [P, W3], F16); wq_l = sb("wq_l", [P, W3], F16)
        we = sb("we", [P, E * P]); we_h = sb("we_h", [P, E * P], F16); we_l = sb("we_l", [P, E * P], F16)
        wr = sb("wr", [P, E]); wr_h = sb("wr_h", [P, E], F16); wr_l = sb("wr_l", [P, E], F16)
        we_last = sb("we_last", [P, E * P])
        wr_last = sb("wr_last", [P, E])
        wo, bo, ln_s = sb("wo", [P, P]), sb("bo", [P, P]), sb("ln_s", [P, P])
        wmax, wgmax, wscale = sb("wmax", [P, 4]), sb("wgmax", [P, 4]), sb("wscale", [P, 4])
        sigma = sb("sigma", [P, 4])
        mean_w = sb("mean_w", [P, 2])

        xa = sb("xa", [P, 4, T * P])
        xc = sb("xc", [P, 4, T * P])
        xn1 = sb("xn1", [P, T * P])
        x1h, x1l = sb("x1h", [P, T * P], F16), sb("x1l", [P, T * P], F16)
        qe = sb("qe", [P, G, T * P])
        qr = sb("qr", [P, G, T * HEADS])
        kv = sb("kv", [P, G, T, KV])
        kmax = sb("kmax", [P, T * P])
        kred, kdiag, kmax_all = sb("kred", [P, P]), sb("kdiag", [P, P]), sb("kmax_all", [P, P])
        kcol = sb("kcol", [P, 1])
        ke = sb("ke", [P, 2, T * P])
        rksum = sb("rksum", [P, 1])
        cn, cnt, mix = sb("cn", [P, P]), sb("cnt", [P, P]), sb("mix", [P, P])
        qn, qt = sb("qn", [P, T * P]), sb("qt", [P, T * P])
        os_ = sb("os_", [P, T * P])
        res = sb("res", [P, T * P])
        x2 = sb("x2", [P, 4, T * P])
        xn2 = sb("xn2", [P, T * P])
        x2h, x2l = sb("x2h", [P, 2, T * P], F16), sb("x2l", [P, 2, T * P], F16)
        qmax, qsum = sb("qmax", [P, T * HEADS]), sb("qsum", [P, T * HEADS])
        st1, st2, st3 = sb("st1", [P, T, 6]), sb("st2", [P, T, 6]), sb("st3", [P, T, 6])
        mv1, mv2, mv3 = sb("mv1", [P, T, 2]), sb("mv2", [P, T, 2]), sb("mv3", [P, T, 2])
        nm1, nm2, nmr2 = sb("nm1", [P, T]), sb("nm2", [P, T]), sb("nmr2", [P, T])
        ln1, ln2, ln3 = sb("ln1", [P, T]), sb("ln2", [P, T]), sb("ln3", [P, T])
        rs1, rs2, rs3 = sb("rs1", [P, T]), sb("rs2", [P, T]), sb("rs3", [P, T])
        logit = sb("logit", [P, T, E])
        top = sb("top", [P, T, 8]); top_i = sb("top_i", [P, T, 8], U32)
        gap, e2, e2p, r2, g1, g2 = (sb(n, [P, T]) for n in ("gap", "e2", "e2p", "r2", "g1", "g2"))
        oh1, oh2 = sb("oh1", [P, T, E]), sb("oh2", [P, T, E])
        gate = sb("gate", [P, 2, T, E])
        acc = sb("acc", [P, 2, T * P])
        prod = sb("prod", [P, 2, HALF, T * P])
        y = sb("y", [P, 2, T * P])
        spare = sb("spare", [P, 2, T * P])

        t0 = ps("t0", [P, 512])
        t1 = ps("t1", [P, 512])
        pq = ps("pq", [P, 3 * 512])
        px = ps("px", [P, 3 * 512])
        o_ps = pq[:, 0:512]
        ctx_ps = pq[:, 1024:1024 + P + 1]

        names = """dve_go pool_go rows w_in w_cast const wmaxed wall wscaled wsplit maskd centred
            st1 aggr1 nm1 ln1 rs1 xn1 x1t hi1 lo1 qkv qmax qsub kv kmax qexp qsum qr
            kred kturn kcol kdiag kspread kall ksub kexp ctx rk cn cturn cnt mixp mix
            qn qt qtc o oc st3 aggr3 ln3 rs3 r3 x2 st2 aggr2 nm2 ln2 rs2 nmr2 xn2
            x2t hi2 lo2 rout logit top gap topi e2 e2p r2 g1 g2 oh ga gb gate
            expv exps acc prod ysum y""".split()
        S = {n: sem("s_" + n) for n in names}
        xa_in = [sem(f"s_xa_in{r}") for r in range(4)]
        xc_in = [sem(f"s_xc_in{r}") for r in range(4)]
        y_out = [sem(f"s_y_out{r}") for r in range(2)]
        N_IN = 7

        block = ctx.enter_context(nc.Block())

        def pieces(t):
            a, end, found = t * W3, (t + 1) * W3, []
            while a < end:
                b = min(end, (a // 512 + 1) * 512)
                found.append((a, a - t * W3, b - a))
                a = b
            return found

        def tiles(ap, cols=P):
            return ap.rearrange("p (t c) -> p t c", t=T)

        q_ps = pq[:, :].rearrange("p (t c) -> p t c", t=T)[:, :, 0:P]
        kv_ps = pq[:, :].rearrange("p (t c) -> p t c", t=T)[:, :, P:W3]

        def unit_bank(u):
            return px[:, (u % 3) * 512:(u % 3 + 1) * 512]

        def iterations(eng, iteration):
            iteration(0, True, False)
            with eng.Fori(1, B) as i:
                iteration(i, True, True)
            iteration(B, False, True)

        @block.sync
        def _(sp):
            sp.dma_start(wq[:, :], w_qkv).then_inc(S["w_in"], 16)
            sp.dma_start(we[:, :].rearrange("c (e n) -> c e n", e=E), expert_w.rearrange("e c n -> c e n")).then_inc(S["w_in"], 16)
            sp.dma_start(wr[:, :], router_w).then_inc(S["w_in"], 16)
            sp.dma_start(we_last[:, :].rearrange("c (e n) -> c e n", e=E),
                         expert_w[:, P - 1, :].partition_broadcast(P)).then_inc(S["w_in"], 16)
            sp.dma_start(wr_last[:, :], router_w[P - 1, :].partition_broadcast(P)).then_inc(S["w_in"], 16)
            sp.dma_start(wo[:, :], w_out).then_inc(S["w_in"], 16)
            sp.dma_start(bo[:, :], b_out.partition_broadcast(P)).then_inc(S["w_in"], 16)
            sp.dma_start(ln_s[:, :], ln_scale.partition_broadcast(P)).then_inc(S["w_in"], 16)
            sp.wait_ge(S["wsplit"], 2)
            sp.dma_start(we[P - 1:P, :], expert_b.rearrange("e n -> (e n)").unsqueeze(0)).then_inc(S["w_cast"], 16)
            sp.dma_start(wr[P - 1:P, :], router_b.unsqueeze(0)).then_inc(S["w_cast"], 16)

            def iteration(i, has_a, has_c):
                for g in range(G):
                    n = i * G + g
                    if has_a:
                        at_least(sp, S["xn1"], n - 3)
                        sp.dma_start(xa[:, g % 4, :], x_v[i, g]).then_inc(xa_in[g % 4], 16)
                    if has_c:
                        at_least(sp, S["x2"], n - 3)
                        sp.dma_start(xc[:, g % 4, :], x_v[i - 1, g]).then_inc(xc_in[g % 4], 16)

            iterations(sp, iteration)

        @block.tensor
        def _(pe):
            mm = nc.tensor.matmul
            pe.wait_ge(S["const"], 4)
            pe.wait_ge(S["rows"], 2)
            pe.wait_ge(S["wsplit"], 8)
            pe.wait_ge(S["centred"], 2)

            def turn(dst, src, t):
                return nc.tensor.transpose(dst[:, t * P:(t + 1) * P], src[:, t * P:(t + 1) * P], ident[:, :])

            def experts(i, d, t):
                r = d % 2
                for half in range(2):
                    u = 2 * t + half
                    prev = u - 3
                    base = i * G + d
                    if prev < 0:
                        prev, base = {-3: 6, -2: 7, -1: 5}[prev], base - 1
                    if prev % 2 == 0:
                        at_least(pe, S["acc"], base * 16 + (prev // 2) * 4 + 4)
                    else:
                        at_least(pe, S["prod"], base * 4 + prev // 2 + 1)
                    w = slice(half * 512, half * 512 + 512)
                    hi, lo = x2h[:, r, t * P:(t + 1) * P], x2l[:, r, t * P:(t + 1) * P]
                    mm(unit_bank(u), hi, we_h[:, w], start=True, stop=False)
                    mm(unit_bank(u), hi, we_l[:, w], start=False, stop=False)
                    mm(unit_bank(u), lo, we_h[:, w], start=False, stop=True).then_inc(S["exps" if half else "expv"], 1)

            def turn_x2(i, g):
                n = i * G + g
                at_least(pe, S["xn2"], n + 1)
                at_least(pe, S["qtc"], n + 2 if g < G - 1 else n + 1)
                for t in range(T):
                    last = turn(t1, xn2, t)
                last.then_inc(S["x2t"], 1)

            def route(i, g):
                n = i * G + g
                at_least(pe, S["hi2"], n + 1)
                at_least(pe, S["lo2"], n + 1)
                at_least(pe, S["logit"], n)
                for t in range(T):
                    hi, lo = x2h[:, g % 2, t * P:(t + 1) * P], x2l[:, g % 2, t * P:(t + 1) * P]
                    o = t0[:, t * E:(t + 1) * E]
                    mm(o, hi, wr_h[:, :], start=True, stop=False)
                    mm(o, hi, wr_l[:, :], start=False, stop=False)
                    last = mm(o, lo, wr_h[:, :], start=False, stop=True)
                last.then_inc(S["rout"], 1)

            def finish_context(i):
                at_least(pe, S["qtc"], i * G + 1)
                pe.wait_ge(S["cn"], i)
                nc.tensor.transpose(t1[:, 0:P], cn[:, :], ident[:, :]).then_inc(S["cturn"], 1)
                pe.wait_ge(S["cnt"], i)
                mm(t1[:, P:2 * P], cnt[:, :], wo[:, :], start=True, stop=True).then_inc(S["mixp"], 1)

            def slot(i, g, has_a, has_c):
                n = i * G + g
                if has_a:
                    at_least(pe, S["xn1"], n + 1)
                    if g == 0:
                        at_least(pe, S["kall"], i)
                        at_least(pe, S["logit"], n)
                    else:
                        at_least(pe, S["logit"], n - 1)
                    at_least(pe, S["lo1"], n)
                    for t in range(T):
                        last = turn(t0, xn1, t)
                    last.then_inc(S["x1t"], 1)
                if has_c:
                    at_least(pe, S["qn"], n + 1)
                    at_least(pe, S["lo2"], n - 1 if g else n)
                    if g == 0:
                        at_least(pe, S["kcol"], i)
                    for t in range(T):
                        last = turn(t1, qn, t)
                    last.then_inc(S["qt"], 1)
                    if g >= 2:
                        experts(i, g - 2, 0)
                    if g == 0:
                        finish_context(i)
                        pe.wait_ge(S["mix"], i)
                    at_least(pe, S["qtc"], n + 1)
                    at_least(pe, S["qsub"], n if has_a else B * G)
                    at_least(pe, S["kv"], n if has_a else B * G)
                    for t in range(T):
                        last = mm(o_ps[:, t * P:(t + 1) * P], qt[:, t * P:(t + 1) * P], mix[:, :], start=True, stop=True)
                    last.then_inc(S["o"], 1)
                    if g >= 1:
                        turn_x2(i, g - 1)
                    if g >= 2:
                        experts(i, g - 2, 1)
                    if g >= 1:
                        if has_a:
                            at_least(pe, S["lo1"], n + 1)
                        route(i, g - 1)
                if has_a:
                    at_least(pe, S["hi1"], n + 1)
                    at_least(pe, S["lo1"], n + 1)
                    at_least(pe, S["qsub"], n)
                    at_least(pe, S["kv"], n)
                    if has_c:
                        at_least(pe, S["oc"], n + 1)
                    for t in range(T):
                        hi, lo = x1h[:, t * P:(t + 1) * P], x1l[:, t * P:(t + 1) * P]
                        for w, start, stop, lhs in ((wq_h, True, False, hi), (wq_l, False, False, hi), (wq_h, False, True, lo)):
                            for at, col, width in pieces(t):
                                last = mm(pq[:, at:at + width], lhs, w[:, col:col + width], start=start, stop=stop)
                    last.then_inc(S["qkv"], 1)
                if has_c and g >= 2:
                    experts(i, g - 2, 2)
                    experts(i, g - 2, 3)

            def add_context(i, g):
                n = i * G + g
                at_least(pe, S["kexp"], n + 1)
                for t in range(T):
                    last = mm(ctx_ps, ke[:, g % 2, t * P:(t + 1) * P], kv[:, g, t, P:2 * P + 1],
                              start=(g == 0 and t == 0), stop=(g == G - 1 and t == T - 1))
                last.then_inc(S["ctx"], 1)

            def tail(i, j, has_a, has_c):
                if has_a and j == 0:
                    at_least(pe, S["kred"], i + 1)
                    at_least(pe, S["lo1"], i * G + G)
                    if has_c:
                        at_least(pe, S["logit"], i * G + G - 1)
                    nc.tensor.transpose(t0[:, 0:P], kred[:, :], ident[:, :]).then_inc(S["kturn"], 1)
                if has_c and j == 0:
                    turn_x2(i, G - 1)
                if has_c:
                    experts(i, G - 2 + j, 0)
                if has_a and j == 0:
                    at_least(pe, S["kdiag"], i + 1)
                    mm(t0[:, P:2 * P], ones[:, :], kdiag[:, :], start=True, stop=True).then_inc(S["kspread"], 1)
                if has_c:
                    experts(i, G - 2 + j, 1)
                    if j == 0:
                        if has_a:
                            at_least(pe, S["kall"], i + 1)
                        route(i, G - 1)
                for h in range(4):
                    if has_a:
                        if j == 0 and h == 0:
                            at_least(pe, S["qsub"], i * G + G)
                            at_least(pe, S["kv"], i * G + G)
                        add_context(i, 4 * j + h)
                    if has_c and h < 2:
                        experts(i, G - 2 + j, 2 + h)

            def iteration(i, has_a, has_c):
                for g in range(G):
                    slot(i, g, has_a, has_c)
                for j in range(TAIL):
                    tail(i, j, has_a, has_c)

            iterations(pe, iteration)

        @block.scalar
        def _(act):
            af = nc.scalar.activation
            nc.scalar.preload_act_table_set("natural_log_exp_and_others")
            act.wait_ge(S["const"], 4)
            act.wait_ge(S["rows"], 2)
            act.wait_ge(S["wsplit"], 8)

            def products(i, d, t):
                n = i * G + d
                at_least(act, S["gate"], n + 1)
                if t == 0:
                    at_least(act, S["ysum"], n - 1)
                at_least(act, S["exps"], n * T + t + 1)
                for e in range(HALF):
                    last = nc.scalar.activation(prod[:, d % 2, e, t * P:(t + 1) * P],
                                                unit_bank(2 * t + 1)[:, e * P:(e + 1) * P], ACT.Copy,
                                                scale=gate[:, d % 2, t, HALF + e:HALF + e + 1])
                last.then_inc(S["prod"], 1)

            def store(i, d):
                n = i * G + d
                at_least(act, S["y"], n + 1)
                act.dma_start(out_v[i - 1, d], y[:, d % 2, :]).then_inc(y_out[d % 2], 16)

            def rstd1_log(i, g):
                at_least(act, S["aggr1"], i * G + g + 1)
                at_least(act, S["xn1"], i * G + g)
                af(ln1[:, :], mv1[:, :, 1], ACT.Ln, bias=eps_ln2[:, 0:1]).then_inc(S["ln1"], 1)

            def rstd1_exp(i, g):
                act.wait_ge(S["ln1"], i * G + g + 1)
                af(rs1[:, :], ln1[:, :], ACT.Exp, bias=ln_xs[:, 0:1], scale=-0.5).then_inc(S["rs1"], 1)

            def split2(i, g):
                n = i * G + g
                at_least(act, S["x2t"], n + 1)
                at_least(act, S["expv"], (n - 1) * T)
                at_least(act, S["exps"], (n - 1) * T)
                nc.scalar.copy(x2h[0:P - 1, g % 2, :], t1[0:P - 1, :]).then_inc(S["hi2"], 1)

            def exp_gap(i, g):
                n = i * G + g
                at_least(act, S["gap"], n + 1)
                at_least(act, S["g2"], n)
                af(e2[:, :], gap[:, :], ACT.Exp, bias=zero_col[:, 0:1], scale=sigma[:, 2:3]).then_inc(S["e2"], 1)

            def slot(i, g, has_a, has_c):
                n = i * G + g
                if has_a:
                    if g == 0:
                        rstd1_log(i, 0)
                        rstd1_exp(i, 0)
                    at_least(act, S["x1t"], n + 1)
                    at_least(act, S["qkv"], n)
                    nc.scalar.copy(x1h[:, :], t0[:, :]).then_inc(S["hi1"], 1)
                if has_c:
                    at_least(act, S["qt"], n + 1)
                    at_least(act, S["o"], n)
                    nc.scalar.copy(qt[:, :], t1[:, :]).then_inc(S["qtc"], 1)
                    if g == 0:
                        act.wait_ge(S["cturn"], i)
                        nc.scalar.copy(cnt[:, :], t1[:, 0:P]).then_inc(S["cnt"], 1)
                    if g >= 2:
                        products(i, g - 2, 0)
                    at_least(act, S["o"], n + 1)
                    at_least(act, S["r3"], n)
                    nc.scalar.copy(os_[:, :], o_ps).then_inc(S["oc"], 1)
                if has_c and g >= 1:
                    split2(i, g - 1)
                if has_a and g < G - 1:
                    rstd1_log(i, g + 1)
                    if has_c and g >= 2:
                        products(i, g - 2, 1)
                    rstd1_exp(i, g + 1)
                elif has_c and g >= 2:
                    products(i, g - 2, 1)
                if has_c:
                    at_least(act, S["aggr3"], n + 1)
                    at_least(act, S["r3"], n)
                    af(ln3[:, :], mv3[:, :, 1], ACT.Ln, bias=eps_ln1[:, 0:1]).then_inc(S["ln3"], 1)
                if has_a:
                    at_least(act, S["qkv"], n + 1)
                    at_least(act, S["ctx"], n - G + 1)
                    nc.scalar.copy(kv[:, g, :, 0:2 * P], kv_ps).then_inc(S["kv"], 1)
                if has_c:
                    act.wait_ge(S["ln3"], n + 1)
                    af(rs3[:, :], ln3[:, :], ACT.Exp, bias=zero_col[:, 0:1], scale=-0.5).then_inc(S["rs3"], 1)
                    if g >= 1:
                        exp_gap(i, g - 1)
                    if g >= 2:
                        products(i, g - 2, 2)
                if has_a:
                    at_least(act, S["qsub"], n + 1)
                    af(qe[:, g, :], qe[:, g, :], ACT.Exp, bias=zero_col[:, 0:1], scale=sigma[:, 0:1]).then_inc(S["qexp"], 1)
                if has_c:
                    at_least(act, S["aggr2"], n + 1)
                    at_least(act, S["xn2"], n)
                    at_least(act, S["nmr2"], n)
                    af(ln2[:, :], mv2[:, :, 1], ACT.Ln, bias=eps_ln1[:, 0:1]).then_inc(S["ln2"], 1)
                    if g >= 2:
                        products(i, g - 2, 3)
                    act.wait_ge(S["ln2"], n + 1)
                    af(rs2[:, :], ln2[:, :], ACT.Exp, bias=ln_xs[:, 0:1], scale=-0.5).then_inc(S["rs2"], 1)
                    act.wait_ge(S["rs2"], n + 1)
                    at_least(act, S["nmr2"], n + 1)
                    at_least(act, S["x2t"], n)
                    for t in range(T):
                        last = af(xn2[:, t * P:(t + 1) * P], x2[:, g % 4, t * P:(t + 1) * P], ACT.Identity,
                                  bias=nmr2[:, t:t + 1], scale=rs2[:, t:t + 1])
                    last.then_inc(S["xn2"], 1)
                    if g >= 3:
                        store(i, g - 3)

            def tail(i, j, has_a, has_c):
                if has_c:
                    if j == 0:
                        split2(i, G - 1)
                    products(i, G - 2 + j, 0)
                if has_a and j == 0:
                    at_least(act, S["kspread"], i + 1)
                    at_least(act, S["ksub"], i * G)
                    nc.scalar.copy(kmax_all[:, :], t0[:, P:2 * P]).then_inc(S["kall"], 1)
                if has_c:
                    products(i, G - 2 + j, 1)
                    if j == 0:
                        exp_gap(i, G - 1)
                for h in range(4):
                    if has_a:
                        g = 4 * j + h
                        n = i * G + g
                        at_least(act, S["ksub"], n + 1)
                        af(ke[:, g % 2, :], ke[:, g % 2, :], ACT.Exp, bias=zero_col[:, 0:1], scale=sigma[:, 0:1]).then_inc(S["kexp"], 1)
                    if has_c and h < 2:
                        products(i, G - 2 + j, 2 + h)
                if has_c:
                    store(i, G - 3 + j)

            def iteration(i, has_a, has_c):
                for g in range(G):
                    slot(i, g, has_a, has_c)
                for j in range(TAIL):
                    tail(i, j, has_a, has_c)
                if has_c:
                    store(i, G - 1)

            iterations(act, iteration)
            for r in range(2):
                act.wait_ge(y_out[r], 16 * (B * G // 2) + 16)

        @block.gpsimd
        def _(pool):
            gp = nc.gpsimd
            gp.memset(ident[:, :], 0.0)
            gp.memset(ones[:, :], 1.0)
            gp.memset(zero_col[:, :], 0.0)
            gp.memset(one_col[:, :], 1.0)
            gp.memset(eps_ln1[:, :], 1e-5)
            gp.memset(eps_ln2[:, :], 1e-6)
            gp.memset(ln_xs[:, :], LN_XS)
            gp.memset(kv[:, :, :, 2 * P:KV], 1.0)
            gp.iota(expert_no_i[:, :, :], pattern=[[0, T], [1, E]], base=0, channel_multiplier=0).then_inc(S["const"], 1)
            pool.wait_ge(S["const"], 1)
            gp.tensor_copy(expert_no[:, :, :], expert_no_i[:, :, :]).then_inc(S["const"], 1)
            gp.affine_select(out=ident[:, :], in_=ident[:, :], compare_op=ALU.not_equal, fill=1.0, base=0,
                             pattern=[[-1, P]], channel_multiplier=1).then_inc(S["const"], 1)
            hm = head_mask[:, :].rearrange("p (h k) -> p h k", h=HEADS)
            gp.affine_select(out=hm, in_=ones[:, :].rearrange("p (h k) -> p h k", h=HEADS), compare_op=ALU.is_ge, fill=0.0,
                             base=0, pattern=[[-DH, HEADS], [0, DH]], channel_multiplier=1).then_inc(S["maskd"], 1)
            pool.wait_ge(S["maskd"], 1)
            gp.affine_select(out=hm, in_=hm, compare_op=ALU.is_ge, fill=0.0,
                             base=DH - 1, pattern=[[DH, HEADS], [0, DH]], channel_multiplier=-1).then_inc(S["const"], 1)
            pool.wait_ge(S["wmaxed"], 3)
            gp.partition_all_reduce(wgmax[:, 0:3], wmax[:, 0:3], P, R_MAX).then_inc(S["wall"], 1)
            for n in "qn x2 nmr2 gate ga gb ysum y".split():
                pool.sem_inc(S[n], G)
            for r in range(2):
                pool.sem_inc(y_out[r], 16)

            def normalise_q(i, g):
                n = i * G + g
                at_least(pool, S["qr"], n - G + 1)
                at_least(pool, S["qt"], n)
                gp.tensor_tensor(qn[:, :].rearrange("p (h k) -> p h k", k=DH), qe[:, g, :].rearrange("p (h k) -> p h k", k=DH),
                                 qr[:, g, :].unsqueeze(2).to_broadcast([P, T * HEADS, DH]), ALU.mult).then_inc(S["qn"], 1)

            def normalise_x1(i, g):
                n = i * G + g
                at_least(pool, S["nm1"], n + 1)
                at_least(pool, S["rs1"], n + 1)
                at_least(pool, S["x1t"], n)
                step_on(pool, S["pool_go"])
                for t in range(T):
                    last = gp.tensor_scalar(xn1[:, t * P:(t + 1) * P], xa[:, g % 4, t * P:(t + 1) * P],
                                            nm1[:, t:t + 1], rs1[:, t:t + 1], ALU.add, ALU.mult)
                last.then_inc(S["xn1"], 1)

            def sum_experts(i, d):
                n, r = i * G + d, d % 2
                at_least(pool, S["acc"], n * 16 + 16)
                at_least(pool, S["prod"], n * 4 + 4)
                at_least(pool, S["y"], n)
                gp.tensor_tensor(spare[:, 0, :], prod[:, r, 0, :], prod[:, r, 1, :], ALU.add)
                gp.tensor_tensor(spare[:, 1, :], prod[:, r, 2, :], prod[:, r, 3, :], ALU.add).then_inc(S["ga"], 1)
                at_least(pool, S["ga"], n + 1)
                gp.tensor_tensor(spare[:, 0, :], spare[:, 0, :], spare[:, 1, :], ALU.add).then_inc(S["ysum"], 1)
                at_least(pool, S["ysum"], n + 1)
                pool.wait_ge(y_out[r], i * 64 + (16 * (d // 2) - 48))
                gp.tensor_tensor(y[:, r, :], spare[:, 0, :], acc[:, r, :], ALU.add).then_inc(S["y"], 1)

            def mix_gates(i, g):
                n = i * G + g
                at_least(pool, S["oh"], n + 1)
                at_least(pool, S["g2"], n + 1)
                spread = lambda v: v[:, :].unsqueeze(2).to_broadcast([P, T, E])
                gp.tensor_tensor(oh1[:, :, :], oh1[:, :, :], spread(g1), ALU.mult)
                gp.tensor_tensor(oh2[:, :, :], oh2[:, :, :], spread(g2), ALU.mult).then_inc(S["gb"], 1)
                at_least(pool, S["gb"], n + 1)
                at_least(pool, S["acc"], n * 16 - 16)
                at_least(pool, S["prod"], n * 4 - 4)
                gp.tensor_tensor(gate[:, g % 2, :, :], oh1[:, :, :], oh2[:, :, :], ALU.add).then_inc(S["gate"], 1)

            def residual(i, g):
                n = i * G + g
                at_least(pool, S["r3"], n + 1)
                pool.wait_ge(xc_in[g % 4], i * 32 + (16 * (g // 4 + 1) - 32))
                at_least(pool, S["acc"], n * 16 - 48)
                at_least(pool, S["xn2"], n - 3)
                gp.tensor_tensor(x2[:, g % 4, :], res[:, :], xc[:, g % 4, :], ALU.add).then_inc(S["x2"], 1)

            def slot(i, g, has_a, has_c):
                n = i * G + g
                if has_a and g == 0:
                    normalise_x1(i, 0)
                if has_c and g < G - 1:
                    normalise_q(i, g + 1)
                if has_c and g >= 3:
                    sum_experts(i, g - 3)
                if has_a and g < G - 1:
                    normalise_x1(i, g + 1)
                if has_c:
                    residual(i, g)
                    if g >= 1:
                        mix_gates(i, g - 1)
                    at_least(pool, S["rs2"], n + 1)
                    at_least(pool, S["nm2"], n + 1)
                    at_least(pool, S["xn2"], n)
                    gp.tensor_tensor(nmr2[:, :], nm2[:, :], rs2[:, :], ALU.mult).then_inc(S["nmr2"], 1)

            def tail(i, j, has_a, has_c):
                for h in range(4):
                    if has_a:
                        g = 4 * j + h
                        n = i * G + g
                        if g == 0:
                            at_least(pool, S["kall"], i + 1)
                            at_least(pool, S["kmax"], n + G)
                        at_least(pool, S["kv"], n + 1)
                        at_least(pool, S["ctx"], n - 1)
                        gp.tensor_tensor(ke[:, g % 2, :].rearrange("p (t c) -> p t c", t=T), kv[:, g, :, 0:P],
                                         kmax_all[:, :].unsqueeze(1).to_broadcast([P, T, P]), ALU.subtract).then_inc(S["ksub"], 1)
                    if has_c and h == 0 and j == 0:
                        mix_gates(i, G - 1)
                    if has_c and h == 2:
                        sum_experts(i, G - 3 + j)

            def iteration(i, has_a, has_c):
                for g in range(G):
                    slot(i, g, has_a, has_c)
                for j in range(TAIL):
                    tail(i, j, has_a, has_c)
                if has_a:
                    normalise_q(i + 1, 0)
                if has_c:
                    sum_experts(i, G - 1)

            iterations(pool, iteration)

        @block.vector
        def _(dve):
            v = nc.vector
            v.memset(x2h[96:P, :, :], XS).then_inc(S["rows"], 1)
            v.memset(x2l[96:P, :, :], 0.0).then_inc(S["rows"], 1)
            dve.wait_ge(S["w_in"], 16 * 8)
            v.tensor_tensor(we[:, :], we[:, :], we_last[:, :], ALU.subtract).then_inc(S["wsplit"], 1)
            v.tensor_tensor(wr[:, :], wr[:, :], wr_last[:, :], ALU.subtract).then_inc(S["wsplit"], 1)
            dve.wait_ge(S["w_cast"], 32)
            for k, w in enumerate((wq, we, wr)):
                v.tensor_reduce(wmax[:, k:k + 1], w[:, :], op=ALU.max, axis=AX_X, apply_absolute_value=True).then_inc(S["wmaxed"], 1)
            v.tensor_reduce(mean_w[:, 0:1], wo[:, :], op=ALU.add, axis=AX_X)
            v.tensor_reduce(mean_w[:, 1:2], bo[:, :], op=ALU.add, axis=AX_X).then_inc(S["wscaled"], 1)
            dve.wait_ge(S["wscaled"], 1)
            v.tensor_scalar(mean_w[:, :], mean_w[:, :], 1.0 / P, None, ALU.mult).then_inc(S["wscaled"], 1)
            dve.wait_ge(S["wscaled"], 2)
            v.tensor_scalar(wo[:, :], wo[:, :], mean_w[:, 0:1], None, ALU.subtract).then_inc(S["centred"], 1)
            v.tensor_scalar(bo[:, :], bo[:, :], mean_w[:, 1:2], 1.0 / HEADS, ALU.subtract, ALU.mult).then_inc(S["centred"], 1)
            dve.wait_ge(S["wall"], 1)
            v.tensor_scalar(wgmax[:, 0:3], wgmax[:, 0:3], 1e-30, None, ALU.max).then_inc(S["wscaled"], 1)
            dve.wait_ge(S["wscaled"], 3)
            v.reciprocal(wscale[:, 0:3], wgmax[:, 0:3]).then_inc(S["wscaled"], 1)
            v.tensor_scalar(sigma[:, 0:3], wgmax[:, 0:3], 1.0 / (WS * XS), None, ALU.mult).then_inc(S["wscaled"], 1)
            dve.wait_ge(S["wscaled"], 5)
            for k, w in enumerate((wq, we, wr)):
                v.tensor_scalar(w[:, :], w[:, :], wscale[:, k:k + 1], WS, ALU.mult, ALU.mult).then_inc(S["wscaled"], 1)
            dve.wait_ge(S["wscaled"], 8)
            for w, hi in ((wq, wq_h), (we, we_h), (wr, wr_h)):
                v.tensor_copy(hi[:, :], w[:, :]).then_inc(S["wsplit"], 1)
            dve.wait_ge(S["wsplit"], 5)
            for w, hi, lo in ((wq, wq_h, wq_l), (we, we_h, we_l), (wr, wr_h, wr_l)):
                v.tensor_tensor(lo[:, :], w[:, :], hi[:, :], ALU.subtract).then_inc(S["wsplit"], 1)
            dve.wait_ge(S["const"], 4)
            v.tensor_scalar(head_mask[:, :], head_mask[:, :], sigma[:, 0:1], DH ** -0.5 / N, ALU.mult, ALU.mult)\
                .then_inc(S["wscaled"], 1)
            dve.wait_ge(S["wscaled"], 9)
            dve.wait_ge(S["rows"], 2)
            dve.wait_ge(S["centred"], 2)

            def mean_var(st, mv, stats_done, mean_done, n):
                dve.wait_ge(stats_done, n)
                step_on(dve, S["dve_go"])
                for t in range(T):
                    last = v.bn_aggr(mv[:, t, :], st[:, t, :])
                last.then_inc(mean_done, 1)

            def stats1(i, g, t):
                if t == 0:
                    dve.wait_ge(xa_in[g % 4], i * 32 + 16 * (g // 4 + 1))
                last = v.bn_stats(st1[:, t, :], xa[:, g % 4, t * P:(t + 1) * P])
                if t == T - 1:
                    last.then_inc(S["st1"], 1)

            def finish_stats1(i, g):
                n = i * G + g
                at_least(dve, S["rs1"], n)
                mean_var(st1, mv1, S["st1"], S["aggr1"], n + 1)
                dve.wait_ge(S["aggr1"], n + 1)
                at_least(dve, S["xn1"], n)
                v.tensor_scalar(nm1[:, :], mv1[:, :, 0], -1.0, None, ALU.mult).then_inc(S["nm1"], 1)

            def weigh(i, d, t, e):
                n = i * G + d
                if e == 0:
                    at_least(dve, S["gate"], n + 1)
                    at_least(dve, S["x2"], n + 1)
                    at_least(dve, S["y"], n - 1)
                    at_least(dve, S["expv"], n * T + t + 1)
                else:
                    dve.wait_ge(S["acc"], n * 16 + t * 4 + e)
                a = acc[:, d % 2, t * P:(t + 1) * P]
                v.scalar_tensor_tensor(out=a, in0=unit_bank(2 * t)[:, e * P:(e + 1) * P],
                                       scalar=gate[:, d % 2, t, e:e + 1],
                                       in1=x2[:, d % 4, t * P:(t + 1) * P] if e == 0 else a,
                                       op0=ALU.mult, op1=ALU.add).then_inc(S["acc"], 1)

            def split2(i, g):
                n = i * G + g
                at_least(dve, S["hi2"], n + 1)
                at_least(dve, S["exps"], (n - 1) * T)
                v.tensor_tensor(x2l[0:P - 1, g % 2, :], t1[0:P - 1, :], x2h[0:P - 1, g % 2, :], ALU.subtract).then_inc(S["lo2"], 1)

            def gates_logit(i, g):
                n = i * G + g
                at_least(dve, S["rout"], n + 1)
                v.tensor_copy(logit[:, :, :], t0[:, 0:T * E].rearrange("p (t e) -> p t e", t=T)).then_inc(S["logit"], 1)

            def gates_top(i, g):
                n = i * G + g
                dve.wait_ge(S["logit"], n + 1)
                step_on(dve, S["dve_go"])
                for t in range(T):
                    last = v.max(top[:, t, :], logit[:, t, :])
                last.then_inc(S["top"], 1)

            def gates_gap(i, g):
                n = i * G + g
                dve.wait_ge(S["top"], n + 1)
                at_least(dve, S["e2"], n)
                v.tensor_tensor(gap[:, :], top[:, :, 1], top[:, :, 0], ALU.subtract).then_inc(S["gap"], 1)
                for t in range(T):
                    last = v.max_index(top_i[:, t, :], top[:, t, :], logit[:, t, :])
                last.then_inc(S["topi"], 1)

            def gates_onehot(i, g, k):
                n = i * G + g
                if k == 0:
                    dve.wait_ge(S["topi"], n + 1)
                    at_least(dve, S["gate"], n)
                last = v.tensor_tensor((oh1, oh2)[k][:, :, :], expert_no[:, :, :],
                                       top_i[:, :, k:k + 1].to_broadcast([P, T, E]), ALU.is_equal)
                if k == 1:
                    last.then_inc(S["oh"], 1)

            def gates_sum(i, g):
                n = i * G + g
                dve.wait_ge(S["e2"], n + 1)
                v.tensor_scalar(e2p[:, :], e2[:, :], 1.0, None, ALU.add).then_inc(S["e2p"], 1)

            def gates_recip(i, g):
                n = i * G + g
                dve.wait_ge(S["e2p"], n + 1)
                v.reciprocal(r2[:, :], e2p[:, :]).then_inc(S["r2"], 1)

            def gates_first(i, g):
                n = i * G + g
                dve.wait_ge(S["r2"], n + 1)
                at_least(dve, S["gb"], n)
                v.tensor_scalar(g1[:, :], r2[:, :], sigma[:, 1:2], None, ALU.mult).then_inc(S["g1"], 1)

            def gates_second(i, g):
                n = i * G + g
                dve.wait_ge(S["g1"], n + 1)
                v.tensor_tensor(g2[:, :], g1[:, :], e2[:, :], ALU.mult).then_inc(S["g2"], 1)

            def finish_context(i):
                dve.wait_ge(S["ctx"], i * G)
                v.reciprocal(rksum[:, :], ctx_ps[:, P:P + 1]).then_inc(S["rk"], 1)
                dve.wait_ge(S["rk"], i)
                v.scalar_tensor_tensor(out=cn[:, :], in0=ctx_ps[:, 0:P], scalar=rksum[:, 0:1], in1=head_mask[:, :],
                                       op0=ALU.mult, op1=ALU.mult).then_inc(S["cn"], 1)
                dve.wait_ge(S["mixp"], i)
                v.tensor_tensor(mix[:, :], t1[:, P:2 * P], bo[:, :], ALU.add).then_inc(S["mix"], 1)

            def slot(i, g, has_a, has_c):
                n = i * G + g
                d = g - 2
                if has_a and g == 0:
                    for t in range(T):
                        stats1(i, 0, t)
                    finish_stats1(i, 0)
                if has_a:
                    at_least(dve, S["hi1"], n + 1)
                    v.tensor_tensor(x1l[:, :], t0[:, :], x1h[:, :], ALU.subtract).then_inc(S["lo1"], 1)
                if has_c and g == 0:
                    finish_context(i)
                for k in range(4):
                    if has_c and d >= 0:
                        weigh(i, d, 0, k)
                    if has_a and g < G - 1:
                        stats1(i, g + 1, k)
                if has_c and g >= 1:
                    split2(i, g - 1)
                if has_c:
                    at_least(dve, S["oc"], n + 1)
                    for t in range(T):
                        last = v.bn_stats(st3[:, t, :], os_[:, t * P:(t + 1) * P])
                    last.then_inc(S["st3"], 1)
                if has_a and g < G - 1:
                    finish_stats1(i, g + 1)
                if has_c:
                    at_least(dve, S["rs3"], n)
                    mean_var(st3, mv3, S["st3"], S["aggr3"], n + 1)
                    if d >= 0:
                        for e in range(HALF):
                            weigh(i, d, 1, e)
                    if g >= 1:
                        gates_logit(i, g - 1)
                if has_a:
                    at_least(dve, S["kv"], n + 1)
                    v.tensor_reduce(qmax[:, :].rearrange("p (t h) -> p t h", t=T),
                                    q_ps.rearrange("p t (h k) -> p t h k", k=DH), op=ALU.max, axis=AX_X).then_inc(S["qmax"], 1)
                if has_c and g >= 1:
                    gates_top(i, g - 1)
                if has_a:
                    dve.wait_ge(S["qmax"], n + 1)
                    at_least(dve, S["qn"], n + 1)
                    v.tensor_tensor(qe[:, g, :].rearrange("p (t h k) -> p t h k", t=T, k=DH),
                                    q_ps.rearrange("p t (h k) -> p t h k", k=DH),
                                    qmax[:, :].rearrange("p (t h) -> p t h", t=T).unsqueeze(3).to_broadcast([P, T, HEADS, DH]),
                                    ALU.subtract).then_inc(S["qsub"], 1)
                if has_c and g >= 1:
                    gates_gap(i, g - 1)
                if has_c:
                    at_least(dve, S["rs3"], n + 1)
                    at_least(dve, S["x2"], n)
                    for t in range(T):
                        last = v.scalar_tensor_tensor(out=res[:, t * P:(t + 1) * P], in0=os_[:, t * P:(t + 1) * P],
                                                      scalar=rs3[:, t:t + 1], in1=ln_s[:, :], op0=ALU.mult, op1=ALU.mult)
                    last.then_inc(S["r3"], 1)
                    if g >= 1:
                        gates_onehot(i, g - 1, 0)
                    if d >= 0:
                        weigh(i, d, 2, 0)
                    if g >= 1:
                        gates_onehot(i, g - 1, 1)
                        gates_sum(i, g - 1)
                    if d >= 0:
                        weigh(i, d, 2, 1)
                    if g >= 1:
                        gates_recip(i, g - 1)
                    if d >= 0:
                        weigh(i, d, 2, 2)
                    if g >= 1:
                        gates_first(i, g - 1)
                    if d >= 0:
                        weigh(i, d, 2, 3)
                    if g >= 1:
                        gates_second(i, g - 1)
                if has_a:
                    k3 = kv[:, g, :, 0:P]
                    km = kmax[:, :].rearrange("p (t c) -> p t c", t=T)
                    if g == 0:
                        v.tensor_copy(km, k3).then_inc(S["kmax"], 1)
                    else:
                        dve.wait_ge(S["kmax"], n)
                        v.tensor_tensor(km, km, k3, ALU.max).then_inc(S["kmax"], 1)
                    at_least(dve, S["qexp"], n + 1)
                    v.tensor_reduce(qsum[:, :], qe[:, g, :].rearrange("p (h k) -> p h k", k=DH), op=ALU.add, axis=AX_X)\
                        .then_inc(S["qsum"], 1)
                if has_c:
                    at_least(dve, S["x2"], n + 1)
                    for t in range(T):
                        last = v.bn_stats(st2[:, t, :], x2[:, g % 4, t * P:(t + 1) * P])
                    last.then_inc(S["st2"], 1)
                if has_a:
                    dve.wait_ge(S["qsum"], n + 1)
                    v.reciprocal(qr[:, g, :], qsum[:, :]).then_inc(S["qr"], 1)
                if has_c:
                    at_least(dve, S["rs2"], n)
                    mean_var(st2, mv2, S["st2"], S["aggr2"], n + 1)
                    if d >= 0:
                        weigh(i, d, 3, 0)
                    dve.wait_ge(S["aggr2"], n + 1)
                    at_least(dve, S["nmr2"], n)
                    v.tensor_scalar(nm2[:, :], mv2[:, :, 0], -1.0, None, ALU.mult).then_inc(S["nm2"], 1)
                    if d >= 0:
                        for e in range(1, HALF):
                            weigh(i, d, 3, e)

            def tail(i, j, has_a, has_c):
                if has_a and j == 0:
                    dve.wait_ge(S["kmax"], i * G + G)
                    at_least(dve, S["kturn"], i)
                    v.tensor_reduce(kred[:, :], kmax[:, :].rearrange("p (t c) -> p c t", t=T), op=ALU.max, axis=AX_X)\
                        .then_inc(S["kred"], 1)
                    dve.wait_ge(S["kturn"], i + 1)
                    v.tensor_reduce(kcol[:, :], t0[:, 0:P], op=ALU.max, axis=AX_X).then_inc(S["kcol"], 1)
                    dve.wait_ge(S["kcol"], i + 1)
                    v.tensor_scalar(kdiag[:, :], ident[:, :], kcol[:, 0:1], None, ALU.mult).then_inc(S["kdiag"], 1)
                if has_c:
                    if j == 0:
                        split2(i, G - 1)
                    for e in range(HALF):
                        weigh(i, G - 2 + j, 0, e)
                    if j == 0:
                        gates_logit(i, G - 1)
                    weigh(i, G - 2 + j, 1, 0)
                    if j == 0:
                        gates_top(i, G - 1)
                    weigh(i, G - 2 + j, 1, 1)
                    if j == 0:
                        gates_gap(i, G - 1)
                    weigh(i, G - 2 + j, 1, 2)
                    if j == 0:
                        gates_onehot(i, G - 1, 0)
                    weigh(i, G - 2 + j, 1, 3)
                    if j == 0:
                        gates_onehot(i, G - 1, 1)
                        gates_sum(i, G - 1)
                    weigh(i, G - 2 + j, 2, 0)
                    if j == 0:
                        gates_recip(i, G - 1)
                    weigh(i, G - 2 + j, 2, 1)
                    if j == 0:
                        gates_first(i, G - 1)
                    weigh(i, G - 2 + j, 2, 2)
                    if j == 0:
                        gates_second(i, G - 1)
                    weigh(i, G - 2 + j, 2, 3)
                    for e in range(HALF):
                        weigh(i, G - 2 + j, 3, e)

            for name in "st3 aggr3 r3 st2 aggr2 nm2 lo2 logit top gap topi oh e2p r2 g1 g2".split():
                dve.sem_inc(S[name], G)
            dve.sem_inc(S["acc"], 16 * G)
            for name in "qt o x2t rout qtc oc ln3 rs3 ln2 rs2 xn2 hi2 e2".split():
                dve.sem_inc(S[name], G)
            dve.sem_inc(S["prod"], T * G)
            dve.sem_inc(S["expv"], T * G)
            dve.sem_inc(S["exps"], T * G)

            def iteration(i, has_a, has_c):
                for g in range(G):
                    slot(i, g, has_a, has_c)
                for j in range(TAIL):
                    tail(i, j, has_a, has_c)

            iterations(dve, iteration)


_INS = ["x", "L0_conv_w_qkv", "L0_conv_w_out", "L0_conv_b_out", "L0_conv_ln_scale",
        "L0_ffn_router_w", "L0_ffn_router_b", "L0_ffn_expert_w", "L0_ffn_expert_b"]


def kernel(**inputs):
    import numpy as _np
    import concourse.bacc as _bacc
    from concourse import mybir as _mybir
    from concourse.bass_utils import run_bass_kernel_spmd as _run

    nc = _bacc.Bacc("TRN2", target_bir_lowering=False, num_devices=1)
    arrays, args = {}, []
    for name in _INS:
        a = _np.ascontiguousarray(inputs[name])
        arrays[f"in_{name}"] = a
        args.append(nc.dram_tensor(f"in_{name}", a.shape, _mybir.dt.from_np(a.dtype), kind="ExternalInput").ap())
    args.append(nc.dram_tensor("out_0", inputs["x"].shape, F32, kind="ExternalOutput").ap())
    metaformer_kernel(nc, *args)
    r = _run(nc, [arrays], core_ids=[0])
    return r.results[0]["out_0"]
```

```python
from contextlib import ExitStack

import concourse.bass as bass
from concourse import mybir

F32, F16, U32, I32 = mybir.dt.float32, mybir.dt.float16, mybir.dt.uint32, mybir.dt.int32
ALU = mybir.AluOpType
ACT = mybir.ActivationFunctionType
AX_X = mybir.AxisListType.X
R_MAX = bass.bass_isa.ReduceOp.max

P = 128
HEADS, DH = 4, 32
E = 8
T = 4
G = 8
BLOCK = 16
W3 = 3 * P
KV = 2 * P + 1
HALF = E // 2
XS = 256.0
WS = 1024.0
LN_XS = 5.545177444479562

LAG = dict(
    stats1=0, xn1=0,
    proj=1, q=1, kmax=1, qsum=2,
    ksub=9, kexp=9, ctx=10,
    qn=17, out=18,
    stats3=19, res=19, x2=20,
    stats2=21, xn2=21,
    route=22, gates=23,
    experts=24, ysum=25,
)


def at_least(eng, sem, value):
    if isinstance(value, int) and value < 1:
        return
    eng.wait_ge(sem, value)


def step_on(eng, going):
    eng.sem_inc(going, 1)


def metaformer_kernel(nc, x, w_qkv, w_out, b_out, ln_scale, router_w, router_b, expert_w, expert_b, out):
    B = x.shape[0]
    N = x.shape[1] * x.shape[2]
    M = B * G
    assert N == G * T * P
    x_v = x.rearrange("b h w c -> (b h w) c").rearrange("(m p t) c -> m p (t c)", m=M, p=P)
    out_v = out.rearrange("b h w c -> (b h w) c").rearrange("(m p t) c -> m p (t c)", m=M, p=P)
    SLOTS = M + LAG["ysum"] + 1
    FILL = 2 * BLOCK
    LOOPS = max(0, M - FILL) // BLOCK

    ctx = ExitStack()
    with ctx:
        def sb(name, shape, dt=F32):
            return ctx.enter_context(nc.sbuf_tensor(name, shape, dt))

        def ps(name, shape):
            return ctx.enter_context(nc.psum_tensor(name, shape, F32))

        def sem(name):
            return ctx.enter_context(nc.semaphore(name))

        ident = sb("ident", [P, P])
        ones = sb("ones", [P, P])
        zero_col, ln_xs = sb("zero_col", [P, 1]), sb("ln_xs", [P, 1])
        eps = sb("eps", [P, 3 * T])
        expert_no = sb("expert_no", [P, T, E])
        expert_no_i = sb("expert_no_i", [P, T, E], I32)
        head_mask = sb("head_mask", [P, P])
        wq = sb("wq", [P, W3]); wq_h = sb("wq_h", [P, W3], F16); wq_l = sb("wq_l", [P, W3], F16)
        we_h = sb("we_h", [P, E * P], F16); we_l = sb("we_l", [P, E * P], F16)
        wr = sb("wr", [P, E]); wr_h = sb("wr_h", [P, E], F16); wr_l = sb("wr_l", [P, E], F16)
        wr_last = sb("wr_last", [P, E])
        wo, bo, ln_s = sb("wo", [P, P]), sb("bo", [P, P]), sb("ln_s", [P, P])
        wmax, wgmax, wscale = sb("wmax", [P, 4]), sb("wgmax", [P, 4]), sb("wscale", [P, 4])
        sigma = sb("sigma", [P, 4])
        mean_w = sb("mean_w", [P, 2])

        xa = sb("xa", [P, 4, T * P])
        xc = sb("xc", [P, 4, T * P])
        st = sb("st", [P, 3 * T, 6])
        sd, sm, s1, s2, sq, var, lnv, rs, nmr = (sb(n, [P, 3 * T]) for n in "sd sm s1 s2 sq var lnv rs nmr".split())
        xn1 = sb("xn1", [P, T * P])
        x1h, x1l = sb("x1h", [P, T * P], F16), sb("x1l", [P, T * P], F16)
        qe = sb("qe", [P, BLOCK, T * P])
        qr = sb("qr", [P, BLOCK, T * HEADS])
        kv = sb("kv", [P, BLOCK, T, KV])
        kmax = sb("kmax", [P, T * P])
        kred, kdiag, kmax_all = sb("kred", [P, P]), sb("kdiag", [P, P]), sb("kmax_all", [P, P])
        kcol = sb("kcol", [P, 1])
        ke = sb("ke", [P, 2, T * P])
        csum = sb("csum", [P, P + 1])
        rksum = sb("rksum", [P, 1])
        cn, cnt, mix = sb("cn", [P, P]), sb("cnt", [P, P]), sb("mix", [P, P])
        qn, qt = sb("qn", [P, 2, T * P]), sb("qt", [P, T * P])
        att = sb("att", [P, 2, T * P])
        res = sb("res", [P, T * P])
        x2 = sb("x2", [P, 8, T * P])
        xn2 = sb("xn2", [P, T * P])
        x2h, x2l = sb("x2h", [P, 4, T * P], F16), sb("x2l", [P, 4, T * P], F16)
        qmax, qsum = sb("qmax", [P, T * HEADS]), sb("qsum", [P, T * HEADS])
        logit = sb("logit", [P, T, E])
        top = sb("top", [P, T, 8]); top_i = sb("top_i", [P, T, 8], U32)
        gap, e2, e2p, r2, g1, g2 = (sb(n, [P, T]) for n in ("gap", "e2", "e2p", "r2", "g1", "g2"))
        oh1, oh2 = sb("oh1", [P, T, E]), sb("oh2", [P, T, E])
        gate = sb("gate", [P, 2, T, E])
        acc = sb("acc", [P, 2, T * P])
        prod = sb("prod", [P, 2, HALF, T * P])
        we = prod[:, 0, 0:2, :].rearrange("p a b -> p (a b)")
        we_last = prod[:, 0, 2:4, :].rearrange("p a b -> p (a b)")

        t0 = ps("t0", [P, 512])
        t1 = ps("t1", [P, 512])
        pq = ps("pq", [P, 3 * 512])
        px = ps("px", [P, 3 * 512])
        o_ps = pq[:, 0:512]
        ctx_ps = t0[:, 0:P + 1]

        names = """dve_go pool_go rows w_in w_cast const wmaxed wall wscaled wsplit maskd centred
            st1 st2 st3 sparts squares var lnv rs nmr xn1 x1t hi1 lo1 qkv qmax qsub kv kmax qexp qsum qr
            kred kturn kcol kdiag kspread kall ksub kexp ctx csum rk cn cturn cnt mixp mix
            qn qt qtc o oc res ress x2 xn2
            x2t hi2 lo2 rout logit top gap topi oh e2 e2p r2 g1 g2 gb gate
            expv exps acc prod pairs ysum y""".split()
        S = {n: sem("s_" + n) for n in names}
        xa_in = [sem(f"s_xa_in{r}") for r in range(4)]
        xc_in = [sem(f"s_xc_in{r}") for r in range(4)]
        y_out = [sem(f"s_y_out{r}") for r in range(2)]

        block = ctx.enter_context(nc.Block())

        def runs(n, step):
            return not isinstance(n, int) or 0 <= n - LAG[step] < M

        def upto(m):
            return min(m + 1, M) if isinstance(m, int) else m + 1

        def all_slots(eng, slot):
            first = min(SLOTS, FILL) if LOOPS else SLOTS
            for n in range(first):
                slot(n, n // BLOCK, n % BLOCK)
            if LOOPS:
                with eng.Fori(FILL // BLOCK, FILL // BLOCK + LOOPS) as i:
                    for g in range(BLOCK):
                        slot(i * BLOCK + g, i, g)
                for n in range(FILL + LOOPS * BLOCK, SLOTS):
                    slot(n, n // BLOCK, n % BLOCK)

        def batch_end(n, b, g, lag):
            if (g - lag) % G != G - 1 or isinstance(n, int) and not 0 <= n - lag < M:
                return None
            return b * (BLOCK // G) + (g - lag + 1) // G

        def pieces(t):
            a, end, found = t * W3, (t + 1) * W3, []
            while a < end:
                z = min(end, (a // 512 + 1) * 512)
                found.append((a, a - t * W3, z - a))
                a = z
            return found

        def tile_of(t):
            return slice(t * P, (t + 1) * P)

        q_ps = pq[:, :].rearrange("p (t c) -> p t c", t=T)[:, :, 0:P]
        kv_ps = pq[:, :].rearrange("p (t c) -> p t c", t=T)[:, :, P:W3]

        def unit_bank(u):
            return px[:, (u % 3) * 512:(u % 3 + 1) * 512]

        @block.sync
        def _(sp):
            sp.dma_start(wq[:, :], w_qkv).then_inc(S["w_in"], 16)
            sp.dma_start(we.rearrange("c (e n) -> c e n", e=E), expert_w.rearrange("e c n -> c e n")).then_inc(S["w_in"], 16)
            sp.dma_start(wr[:, :], router_w).then_inc(S["w_in"], 16)
            sp.dma_start(we_last.rearrange("c (e n) -> c e n", e=E),
                         expert_w[:, P - 1, :].partition_broadcast(P)).then_inc(S["w_in"], 16)
            sp.dma_start(wr_last[:, :], router_w[P - 1, :].partition_broadcast(P)).then_inc(S["w_in"], 16)
            sp.dma_start(wo[:, :], w_out).then_inc(S["w_in"], 16)
            sp.dma_start(bo[:, :], b_out.partition_broadcast(P)).then_inc(S["w_in"], 16)
            sp.dma_start(ln_s[:, :], ln_scale.partition_broadcast(P)).then_inc(S["w_in"], 16)
            sp.wait_ge(S["wsplit"], 2)
            sp.dma_start(we[P - 1:P, :], expert_b.rearrange("e n -> (e n)").unsqueeze(0)).then_inc(S["w_cast"], 16)
            sp.dma_start(wr[P - 1:P, :], router_b.unsqueeze(0)).then_inc(S["w_cast"], 16)

            def slot(n, b, g):
                if runs(n, "stats1"):
                    at_least(sp, S["xn1"], n - 3)
                    sp.dma_start(xa[:, g % 4, :], x_v[n]).then_inc(xa_in[g % 4], 16)
                if runs(n + 2, "x2"):
                    m, r = n + 2 - LAG["x2"], (g + 2 - LAG["x2"]) % 4
                    at_least(sp, S["x2"], m - 3)
                    sp.dma_start(xc[:, r, :], x_v[m]).then_inc(xc_in[r], 16)

            all_slots(sp, slot)

        @block.tensor
        def _(pe):
            mm = nc.tensor.matmul
            pe.wait_ge(S["const"], 4)
            pe.wait_ge(S["rows"], 3)
            pe.wait_ge(S["wsplit"], 8)
            pe.wait_ge(S["centred"], 2)

            def turn(dst, src, t):
                return nc.tensor.transpose(dst[:, tile_of(t)], src[:, tile_of(t)], ident[:, :])

            def experts(n, g, t):
                if not runs(n, "experts"):
                    return
                m, r = n - LAG["experts"], (g - LAG["experts"]) % 4
                hi, lo = x2h[:, r, tile_of(t)], x2l[:, r, tile_of(t)]
                for half in range(2):
                    u = 2 * t + half
                    had, of = (u - 3, m) if u >= 3 else ((6, 7, 5)[u], m - 1)
                    if had % 2 == 0:
                        at_least(pe, S["acc"], of * 16 + (had // 2) * 4 + 4)
                    else:
                        at_least(pe, S["prod"], of * 4 + had // 2 + 1)
                    w = slice(half * 512, half * 512 + 512)
                    mm(unit_bank(u), hi, we_h[:, w], start=True, stop=False)
                    mm(unit_bank(u), hi, we_l[:, w], start=False, stop=False)
                    mm(unit_bank(u), lo, we_h[:, w], start=False, stop=True).then_inc(S["exps" if half else "expv"], 1)

            def turn_x1(n, g):
                if runs(n, "proj"):
                    m = n - LAG["proj"]
                    at_least(pe, S["xn1"], m + 1)
                    at_least(pe, S["lo1"], m)
                    at_least(pe, S["csum"], upto(n - 1 - LAG["ctx"]))
                    for t in range(T):
                        last = turn(t0, xn1, t)
                    last.then_inc(S["x1t"], 1)

            def project(n, g):
                if runs(n, "proj"):
                    m = n - LAG["proj"]
                    at_least(pe, S["hi1"], m + 1)
                    at_least(pe, S["lo1"], m + 1)
                    at_least(pe, S["qsub"], m)
                    at_least(pe, S["kv"], m)
                    at_least(pe, S["oc"], upto(n - LAG["out"]))
                    for t in range(T):
                        hi, lo = x1h[:, tile_of(t)], x1l[:, tile_of(t)]
                        for w, start, stop, lhs in ((wq_h, True, False, hi), (wq_l, False, False, hi), (wq_h, False, True, lo)):
                            for at, col, width in pieces(t):
                                last = mm(pq[:, at:at + width], lhs, w[:, col:col + width], start=start, stop=stop)
                    last.then_inc(S["qkv"], 1)

            def turn_q(n, g):
                if runs(n, "out"):
                    m = n - LAG["out"]
                    at_least(pe, S["qn"], m + 1)
                    at_least(pe, S["logit"], n - LAG["route"])
                    for t in range(T):
                        last = turn(t1, qn[:, (g - LAG["out"]) % 2, :], t)
                    last.then_inc(S["qt"], 1)

            def attend(n, b, g):
                if runs(n, "out"):
                    m = n - LAG["out"]
                    done = batch_end(n - 1, b, g - 1, LAG["ctx"])
                    if done is not None:
                        pe.wait_ge(S["mix"], done)
                    at_least(pe, S["qtc"], m + 1)
                    at_least(pe, S["qsub"], upto(n - 1 - LAG["proj"]))
                    at_least(pe, S["kv"], upto(n - 1 - LAG["proj"]))
                    for t in range(T):
                        last = mm(o_ps[:, tile_of(t)], qt[:, tile_of(t)], mix[:, :], start=True, stop=True)
                    last.then_inc(S["o"], 1)

            def turn_x2(n, g):
                if runs(n, "route"):
                    m = n - LAG["route"]
                    at_least(pe, S["xn2"], m + 1)
                    at_least(pe, S["qtc"], upto(n - LAG["out"]))
                    at_least(pe, S["logit"], m)
                    for t in range(T):
                        last = turn(t1, xn2, t)
                    last.then_inc(S["x2t"], 1)

            def route(n, g):
                if runs(n, "route"):
                    m, r = n - LAG["route"], (g - LAG["route"]) % 4
                    at_least(pe, S["hi2"], m + 1)
                    at_least(pe, S["lo2"], m + 1)
                    for t in range(T):
                        hi, lo = x2h[:, r, tile_of(t)], x2l[:, r, tile_of(t)]
                        o = t1[:, t * E:(t + 1) * E]
                        mm(o, hi, wr_h[:, :], start=True, stop=False)
                        mm(o, hi, wr_l[:, :], start=False, stop=False)
                        last = mm(o, lo, wr_h[:, :], start=False, stop=True)
                    last.then_inc(S["rout"], 1)

            def add_context(n, g):
                if runs(n, "ctx"):
                    m, r = n - LAG["ctx"], (g - LAG["ctx"]) % BLOCK
                    at_least(pe, S["kexp"], m + 1)
                    at_least(pe, S["lo1"], upto(n - LAG["proj"]))
                    for t in range(T):
                        last = mm(ctx_ps, ke[:, r % 2, tile_of(t)], kv[:, r, t, P:KV], start=(t == 0), stop=(t == T - 1))
                    last.then_inc(S["ctx"], 1)

            def turn_kmax(n, b, g):
                done = batch_end(n - 1, b, g - 1, LAG["kmax"])
                if done is not None:
                    pe.wait_ge(S["kred"], done)
                    at_least(pe, S["lo1"], upto(n - LAG["proj"]))
                    nc.tensor.transpose(t0[:, 0:P], kred[:, :], ident[:, :]).then_inc(S["kturn"], 1)

            def spread_kmax(n, b, g):
                done = batch_end(n - 1, b, g - 1, LAG["kmax"])
                if done is not None:
                    pe.wait_ge(S["kdiag"], done)
                    mm(t0[:, P:2 * P], ones[:, :], kdiag[:, :], start=True, stop=True).then_inc(S["kspread"], 1)
                    pe.wait_ge(S["kall"], done)

            def turn_context(n, b, g):
                done = batch_end(n, b, g, LAG["ctx"])
                if done is not None:
                    pe.wait_ge(S["cn"], done)
                    nc.tensor.transpose(t0[:, 0:P], cn[:, :], ident[:, :]).then_inc(S["cturn"], 1)

            def mix_context(n, b, g):
                done = batch_end(n - 1, b, g - 1, LAG["ctx"])
                if done is not None:
                    pe.wait_ge(S["cnt"], done)
                    mm(t0[:, 0:P], cnt[:, :], wo[:, :], start=True, stop=True).then_inc(S["mixp"], 1)
                    pe.wait_ge(S["mix"], done)

            def slot(n, b, g):
                mix_context(n, b, g)
                experts(n, g, 0)
                turn_x1(n, g)
                turn_q(n, g)
                experts(n, g, 1)
                turn_kmax(n, b, g)
                turn_x2(n, g)
                attend(n, b, g)
                spread_kmax(n, b, g)
                experts(n, g, 2)
                add_context(n, g)
                route(n, g)
                project(n, g)
                turn_context(n, b, g)
                experts(n, g, 3)

            all_slots(pe, slot)

        @block.scalar
        def _(act):
            af = nc.scalar.activation
            nc.scalar.preload_act_table_set("natural_log_exp_and_others")
            act.wait_ge(S["const"], 4)
            act.wait_ge(S["rows"], 3)
            act.wait_ge(S["wsplit"], 8)

            def products(n, g, t):
                if not runs(n, "experts"):
                    return
                m, r = n - LAG["experts"], (g - LAG["experts"]) % 2
                at_least(act, S["gate"], m + 1)
                if t == 0:
                    at_least(act, S["ysum"], m - 1)
                at_least(act, S["exps"], m * T + t + 1)
                for e in range(HALF):
                    last = af(prod[:, r, e, tile_of(t)], unit_bank(2 * t + 1)[:, e * P:(e + 1) * P], ACT.Copy,
                              scale=gate[:, r, t, HALF + e:HALF + e + 1])
                last.then_inc(S["prod"], 1)

            def store(n, g):
                if runs(n, "ysum"):
                    m, r = n - LAG["ysum"], (g - LAG["ysum"]) % 2
                    at_least(act, S["y"], m + 1)
                    act.dma_start(out_v[m], acc[:, r, :]).then_inc(y_out[r], 16)

            def split1(n, g):
                if runs(n, "proj"):
                    m = n - LAG["proj"]
                    at_least(act, S["x1t"], m + 1)
                    at_least(act, S["qkv"], m)
                    nc.scalar.copy(x1h[:, :], t0[:, :]).then_inc(S["hi1"], 1)

            def copy_qt(n, g):
                if runs(n, "out"):
                    m = n - LAG["out"]
                    at_least(act, S["qt"], m + 1)
                    at_least(act, S["o"], m)
                    nc.scalar.copy(qt[:, :], t1[:, :]).then_inc(S["qtc"], 1)

            def copy_att(n, g):
                if runs(n, "out"):
                    m, r = n - LAG["out"], (g - LAG["out"]) % 2
                    at_least(act, S["o"], m + 1)
                    at_least(act, S["st3"], m - 1)
                    nc.scalar.copy(att[:, r, :], o_ps).then_inc(S["oc"], 1)

            def split2(n, g):
                if runs(n, "route"):
                    m, r = n - LAG["route"], (g - LAG["route"]) % 4
                    at_least(act, S["x2t"], m + 1)
                    at_least(act, S["expv"], (m - 3) * T)
                    at_least(act, S["exps"], (m - 3) * T)
                    nc.scalar.copy(x2h[0:P - 1, r, :], t1[0:P - 1, :]).then_inc(S["hi2"], 1)

            def rstd_log(n):
                at_least(act, S["var"], n + 1)
                af(lnv[:, :], var[:, :], ACT.Ln, bias=zero_col[:, 0:1]).then_inc(S["lnv"], 1)

            def rstd_exp(n):
                at_least(act, S["lnv"], n + 1)
                at_least(act, S["xn1"], upto(n - 1 - LAG["xn1"]))
                at_least(act, S["nmr"], n)
                af(rs[:, :], lnv[:, :], ACT.Exp, bias=ln_xs[:, 0:1], scale=-0.5).then_inc(S["rs"], 1)

            def scale_att(n, g):
                if runs(n, "res"):
                    m, r = n - LAG["res"], (g - LAG["res"]) % 2
                    at_least(act, S["rs"], n + 1)
                    at_least(act, S["x2"], m)
                    for t in range(T):
                        last = af(res[:, tile_of(t)], att[:, r, tile_of(t)], ACT.Copy, scale=rs[:, T + t:T + t + 1])
                    last.then_inc(S["res"], 1)

            def normalise_x2(n, g):
                if runs(n, "xn2"):
                    m, r = n - LAG["xn2"], (g - LAG["xn2"]) % 8
                    at_least(act, S["nmr"], n + 1)
                    at_least(act, S["x2t"], m)
                    for t in range(T):
                        last = af(xn2[:, tile_of(t)], x2[:, r, tile_of(t)], ACT.Identity,
                                  bias=nmr[:, 2 * T + t:2 * T + t + 1], scale=rs[:, 2 * T + t:2 * T + t + 1])
                    last.then_inc(S["xn2"], 1)

            def copy_kv(n, g):
                if runs(n, "proj"):
                    m, r = n - LAG["proj"], (g - LAG["proj"]) % BLOCK
                    at_least(act, S["qkv"], m + 1)
                    at_least(act, S["ctx"], m - BLOCK + 1)
                    nc.scalar.copy(kv[:, r, :, 0:2 * P], kv_ps).then_inc(S["kv"], 1)

            def exp_q(n, g):
                if runs(n, "q"):
                    m, r = n - LAG["q"], (g - LAG["q"]) % BLOCK
                    at_least(act, S["qsub"], m + 1)
                    af(qe[:, r, :], qe[:, r, :], ACT.Exp, bias=zero_col[:, 0:1], scale=sigma[:, 0:1]).then_inc(S["qexp"], 1)

            def exp_k(n, g):
                if runs(n, "kexp"):
                    m, r = n - LAG["kexp"], (g - LAG["kexp"]) % 2
                    at_least(act, S["ksub"], m + 1)
                    af(ke[:, r, :], ke[:, r, :], ACT.Exp, bias=zero_col[:, 0:1], scale=sigma[:, 0:1]).then_inc(S["kexp"], 1)

            def exp_gap(n, g):
                if runs(n, "gates"):
                    m = n - LAG["gates"]
                    at_least(act, S["gap"], m + 1)
                    at_least(act, S["g2"], m)
                    af(e2[:, :], gap[:, :], ACT.Exp, bias=zero_col[:, 0:1], scale=sigma[:, 2:3]).then_inc(S["e2"], 1)

            def copy_kmax(n, b, g):
                done = batch_end(n - 1, b, g - 1, LAG["kmax"])
                if done is not None:
                    pool_done = n - LAG["ksub"]
                    act.wait_ge(S["kspread"], done)
                    at_least(act, S["ksub"], pool_done)
                    nc.scalar.copy(kmax_all[:, :], t0[:, P:2 * P]).then_inc(S["kall"], 1)

            def copy_context(n, b, g):
                done = batch_end(n, b, g, LAG["ctx"])
                if done is not None:
                    act.wait_ge(S["cturn"], done)
                    nc.scalar.copy(cnt[:, :], t0[:, 0:P]).then_inc(S["cnt"], 1)

            def slot(n, b, g):
                exp_gap(n, g)
                products(n, g, 0)
                split1(n, g)
                copy_qt(n, g)
                products(n, g, 1)
                split2(n, g)
                copy_att(n, g)
                copy_kmax(n, b, g)
                rstd_log(n)
                products(n, g, 2)
                rstd_exp(n)
                scale_att(n, g)
                normalise_x2(n, g)
                copy_kv(n, g)
                exp_k(n, g)
                copy_context(n, b, g)
                products(n, g, 3)
                exp_q(n, g)
                store(n, g)

            all_slots(act, slot)
            for r in range(2):
                act.wait_ge(y_out[r], 16 * (M // 2))

        @block.gpsimd
        def _(pool):
            gp = nc.gpsimd
            gp.memset(ident[:, :], 0.0)
            gp.memset(ones[:, :], 1.0)
            gp.memset(zero_col[:, :], 0.0)
            gp.memset(eps[:, 0:T], 1e-6)
            gp.memset(eps[:, T:3 * T], 1e-5)
            gp.memset(ln_xs[:, :], LN_XS)
            gp.memset(kv[:, :, :, 2 * P:KV], 1.0)
            gp.iota(expert_no_i[:, :, :], pattern=[[0, T], [1, E]], base=0, channel_multiplier=0).then_inc(S["const"], 1)
            pool.wait_ge(S["const"], 1)
            gp.tensor_copy(expert_no[:, :, :], expert_no_i[:, :, :]).then_inc(S["const"], 1)
            gp.affine_select(out=ident[:, :], in_=ident[:, :], compare_op=ALU.not_equal, fill=1.0, base=0,
                             pattern=[[-1, P]], channel_multiplier=1).then_inc(S["const"], 1)
            hm = head_mask[:, :].rearrange("p (h k) -> p h k", h=HEADS)
            gp.affine_select(out=hm, in_=ones[:, :].rearrange("p (h k) -> p h k", h=HEADS), compare_op=ALU.is_ge, fill=0.0,
                             base=0, pattern=[[-DH, HEADS], [0, DH]], channel_multiplier=1).then_inc(S["maskd"], 1)
            pool.wait_ge(S["maskd"], 1)
            gp.affine_select(out=hm, in_=hm, compare_op=ALU.is_ge, fill=0.0,
                             base=DH - 1, pattern=[[DH, HEADS], [0, DH]], channel_multiplier=-1).then_inc(S["const"], 1)
            pool.wait_ge(S["wmaxed"], 3)
            gp.partition_all_reduce(wgmax[:, 0:3], wmax[:, 0:3], P, R_MAX).then_inc(S["wall"], 1)
            pool.wait_ge(S["centred"], 3)

            def normalise_q(n, g):
                if runs(n, "qn"):
                    m, r = n - LAG["qn"], (g - LAG["qn"]) % BLOCK
                    at_least(pool, S["qr"], m + 1)
                    at_least(pool, S["qt"], m - 1)
                    gp.tensor_tensor(qn[:, r % 2, :].rearrange("p (h k) -> p h k", k=DH),
                                     qe[:, r, :].rearrange("p (h k) -> p h k", k=DH),
                                     qr[:, r, :].unsqueeze(2).to_broadcast([P, T * HEADS, DH]), ALU.mult).then_inc(S["qn"], 1)

            def normalise_x1(n, g):
                if runs(n, "xn1"):
                    m, r = n - LAG["xn1"], (g - LAG["xn1"]) % 4
                    at_least(pool, S["nmr"], n + 1)
                    at_least(pool, S["x1t"], m)
                    step_on(pool, S["pool_go"])
                    for t in range(T):
                        last = gp.tensor_scalar(xn1[:, tile_of(t)], xa[:, r, tile_of(t)],
                                                rs[:, t:t + 1], nmr[:, t:t + 1], ALU.mult, ALU.add)
                    last.then_inc(S["xn1"], 1)

            def residual(n, g):
                if runs(n, "x2"):
                    m, r = n - LAG["x2"], g - LAG["x2"]
                    at_least(pool, S["res"], m + 1)
                    gp.tensor_tensor(res[:, :].rearrange("p (t c) -> p t c", t=T), res[:, :].rearrange("p (t c) -> p t c", t=T),
                                     ln_s[:, :].unsqueeze(1).to_broadcast([P, T, P]), ALU.mult).then_inc(S["ress"], 1)

            def residual_sum(n, b, g):
                if runs(n, "x2"):
                    m, r = n - LAG["x2"], g - LAG["x2"]
                    at_least(pool, S["ress"], m + 1)
                    pool.wait_ge(xc_in[r % 4], b * (BLOCK // 4 * 16) + (r // 4 + 1) * 16)
                    at_least(pool, S["acc"], (m - 7) * 16)
                    gp.tensor_tensor(x2[:, r % 8, :], res[:, :], xc[:, r % 4, :], ALU.add).then_inc(S["x2"], 1)

            def sum_pairs(n, g):
                if runs(n, "ysum"):
                    m, r = n - LAG["ysum"], (g - LAG["ysum"]) % 2
                    at_least(pool, S["prod"], m * T + T)
                    gp.tensor_tensor(prod[:, r, 0, :], prod[:, r, 0, :], prod[:, r, 1, :], ALU.add)
                    gp.tensor_tensor(prod[:, r, 2, :], prod[:, r, 2, :], prod[:, r, 3, :], ALU.add).then_inc(S["pairs"], 1)

            def sum_products(n, g):
                if runs(n, "ysum"):
                    m, r = n - LAG["ysum"], (g - LAG["ysum"]) % 2
                    at_least(pool, S["pairs"], m + 1)
                    gp.tensor_tensor(prod[:, r, 0, :], prod[:, r, 0, :], prod[:, r, 2, :], ALU.add).then_inc(S["ysum"], 1)

            def sum_output(n, g):
                if runs(n, "ysum"):
                    m, r = n - LAG["ysum"], (g - LAG["ysum"]) % 2
                    at_least(pool, S["acc"], m * 16 + 16)
                    at_least(pool, S["ysum"], m + 1)
                    gp.tensor_tensor(acc[:, r, :], acc[:, r, :], prod[:, r, 0, :], ALU.add).then_inc(S["y"], 1)

            def weigh_onehots(n, g):
                if runs(n, "gates"):
                    m = n - LAG["gates"]
                    at_least(pool, S["oh"], m + 1)
                    at_least(pool, S["g2"], m + 1)
                    gp.tensor_tensor(oh1[:, :, :], oh1[:, :, :], g1[:, :].unsqueeze(2).to_broadcast([P, T, E]), ALU.mult)
                    gp.tensor_tensor(oh2[:, :, :], oh2[:, :, :], g2[:, :].unsqueeze(2).to_broadcast([P, T, E]), ALU.mult)\
                        .then_inc(S["gb"], 1)

            def sum_gates(n, g):
                if runs(n, "gates"):
                    m, r = n - LAG["gates"], (g - LAG["gates"]) % 2
                    at_least(pool, S["gb"], m + 1)
                    at_least(pool, S["acc"], (m - 1) * 16)
                    at_least(pool, S["prod"], (m - 1) * T)
                    gp.tensor_tensor(gate[:, r, :, :], oh1[:, :, :], oh2[:, :, :], ALU.add).then_inc(S["gate"], 1)

            def subtract_kmax(n, b, g):
                if runs(n, "ksub"):
                    m, r = n - LAG["ksub"], (g - LAG["ksub"]) % BLOCK
                    done = batch_end(n - 1, b, g - 1, LAG["kmax"])
                    if done is not None:
                        pool.wait_ge(S["kall"], done)
                    at_least(pool, S["kv"], m + 1)
                    at_least(pool, S["ctx"], m - 1)
                    gp.tensor_tensor(ke[:, r % 2, :].rearrange("p (t c) -> p t c", t=T), kv[:, r, :, 0:P],
                                     kmax_all[:, :].unsqueeze(1).to_broadcast([P, T, P]), ALU.subtract).then_inc(S["ksub"], 1)

            def slot(n, b, g):
                normalise_q(n, g)
                residual(n, g)
                sum_pairs(n, g)
                residual_sum(n, b, g)
                sum_products(n, g)
                weigh_onehots(n, g)
                subtract_kmax(n, b, g)
                sum_output(n, g)
                sum_gates(n, g)
                normalise_x1(n, g)

            all_slots(pool, slot)

        @block.vector
        def _(dve):
            v = nc.vector
            v.memset(x2h[96:P, :, :], XS).then_inc(S["rows"], 1)
            v.memset(x2l[96:P, :, :], 0.0).then_inc(S["rows"], 1)
            v.memset(st[:, :, :], 0.0).then_inc(S["rows"], 1)
            dve.wait_ge(S["w_in"], 16 * 8)
            v.tensor_tensor(we, we, we_last, ALU.subtract).then_inc(S["wsplit"], 1)
            v.tensor_tensor(wr[:, :], wr[:, :], wr_last[:, :], ALU.subtract).then_inc(S["wsplit"], 1)
            dve.wait_ge(S["w_cast"], 32)
            for k, w in enumerate((wq[:, :], we, wr[:, :])):
                v.tensor_reduce(wmax[:, k:k + 1], w, op=ALU.max, axis=AX_X, apply_absolute_value=True).then_inc(S["wmaxed"], 1)
            v.tensor_reduce(mean_w[:, 0:1], wo[:, :], op=ALU.add, axis=AX_X)
            v.tensor_reduce(mean_w[:, 1:2], bo[:, :], op=ALU.add, axis=AX_X).then_inc(S["wscaled"], 1)
            dve.wait_ge(S["wscaled"], 1)
            v.tensor_scalar(mean_w[:, :], mean_w[:, :], 1.0 / P, None, ALU.mult).then_inc(S["wscaled"], 1)
            dve.wait_ge(S["wscaled"], 2)
            v.tensor_scalar(wo[:, :], wo[:, :], mean_w[:, 0:1], None, ALU.subtract).then_inc(S["centred"], 1)
            v.tensor_scalar(bo[:, :], bo[:, :], mean_w[:, 1:2], 1.0 / HEADS, ALU.subtract, ALU.mult).then_inc(S["centred"], 1)
            v.tensor_scalar(ln_s[:, :], ln_s[:, :], 1.0 / XS, None, ALU.mult).then_inc(S["centred"], 1)
            dve.wait_ge(S["wall"], 1)
            v.tensor_scalar(wgmax[:, 0:3], wgmax[:, 0:3], 1e-30, None, ALU.max).then_inc(S["wscaled"], 1)
            dve.wait_ge(S["wscaled"], 3)
            v.reciprocal(wscale[:, 0:3], wgmax[:, 0:3]).then_inc(S["wscaled"], 1)
            v.tensor_scalar(sigma[:, 0:3], wgmax[:, 0:3], 1.0 / (WS * XS), None, ALU.mult).then_inc(S["wscaled"], 1)
            dve.wait_ge(S["wscaled"], 5)
            for k, w in enumerate((wq[:, :], we, wr[:, :])):
                v.tensor_scalar(w, w, wscale[:, k:k + 1], WS, ALU.mult, ALU.mult).then_inc(S["wscaled"], 1)
            dve.wait_ge(S["wscaled"], 8)
            for w, hi in ((wq[:, :], wq_h), (we, we_h), (wr[:, :], wr_h)):
                v.tensor_copy(hi[:, :], w).then_inc(S["wsplit"], 1)
            dve.wait_ge(S["wsplit"], 5)
            for w, hi, lo in ((wq[:, :], wq_h, wq_l), (we, we_h, we_l), (wr[:, :], wr_h, wr_l)):
                v.tensor_tensor(lo[:, :], w, hi[:, :], ALU.subtract).then_inc(S["wsplit"], 1)
            dve.wait_ge(S["const"], 4)
            v.tensor_scalar(head_mask[:, :], head_mask[:, :], sigma[:, 0:1], DH ** -0.5 / N, ALU.mult, ALU.mult)\
                .then_inc(S["wscaled"], 1)
            dve.wait_ge(S["wscaled"], 9)
            dve.wait_ge(S["rows"], 3)
            dve.wait_ge(S["centred"], 3)

            def stats1(n, b, g, t):
                if runs(n, "stats1"):
                    if t == 0:
                        at_least(dve, S["squares"], n)
                        dve.wait_ge(xa_in[g % 4], b * (BLOCK // 4 * 16) + (g // 4 + 1) * 16)
                    last = v.bn_stats(st[:, t, :], xa[:, g % 4, tile_of(t)])
                    if t == T - 1:
                        last.then_inc(S["st1"], 1)

            def stats3(n, g, t):
                if runs(n, "stats3"):
                    m, r = n - LAG["stats3"], (g - LAG["stats3"]) % 2
                    if t == 0:
                        at_least(dve, S["oc"], m + 1)
                        at_least(dve, S["squares"], n)
                    last = v.bn_stats(st[:, T + t, :], att[:, r, tile_of(t)])
                    if t == T - 1:
                        last.then_inc(S["st3"], 1)

            def stats2(n, g, t):
                if runs(n, "stats2"):
                    m, r = n - LAG["stats2"], (g - LAG["stats2"]) % 8
                    if t == 0:
                        at_least(dve, S["x2"], m + 1)
                        at_least(dve, S["squares"], n)
                    last = v.bn_stats(st[:, 2 * T + t, :], x2[:, r, tile_of(t)])
                    if t == T - 1:
                        last.then_inc(S["st2"], 1)

            def moments_parts(n):
                at_least(dve, S["st1"], upto(n - LAG["stats1"]))
                at_least(dve, S["st3"], upto(n - LAG["stats3"]))
                at_least(dve, S["st2"], upto(n - LAG["stats2"]))
                at_least(dve, S["nmr"], n)
                v.tensor_tensor(sd[:, :], st[:, :, 1], st[:, :, 4], ALU.subtract)
                v.tensor_tensor(sm[:, :], st[:, :, 1], st[:, :, 4], ALU.add)
                v.scalar_tensor_tensor(out=s1[:, :], in0=st[:, :, 2], scalar=1.0 / P, in1=eps[:, :],
                                       op0=ALU.mult, op1=ALU.add).then_inc(S["sparts"], 1)

            def moments_squares(n):
                dve.wait_ge(S["sparts"], n + 1)
                at_least(dve, S["var"], n)
                v.scalar_tensor_tensor(out=sq[:, :], in0=sd[:, :], scalar=0.25, in1=sd[:, :], op0=ALU.mult, op1=ALU.mult)
                v.scalar_tensor_tensor(out=s2[:, :], in0=st[:, :, 5], scalar=1.0 / P, in1=s1[:, :],
                                       op0=ALU.mult, op1=ALU.add).then_inc(S["squares"], 1)

            def moments_var(n):
                dve.wait_ge(S["squares"], n + 1)
                at_least(dve, S["lnv"], n)
                v.tensor_tensor(var[:, :], sq[:, :], s2[:, :], ALU.add).then_inc(S["var"], 1)

            def moments_mean(n):
                at_least(dve, S["rs"], n + 1)
                at_least(dve, S["xn1"], upto(n - 1 - LAG["xn1"]))
                at_least(dve, S["xn2"], upto(n - 1 - LAG["xn2"]))
                v.scalar_tensor_tensor(out=nmr[:, :], in0=sm[:, :], scalar=-0.5, in1=rs[:, :],
                                       op0=ALU.mult, op1=ALU.mult).then_inc(S["nmr"], 1)

            def weigh(n, g, t, e):
                if not runs(n, "experts"):
                    return
                m, r = n - LAG["experts"], (g - LAG["experts"]) % 8
                if e == 0:
                    at_least(dve, S["gate"], m + 1)
                    if t == 0:
                        at_least(dve, S["x2"], m + 1)
                        if isinstance(m, int):
                            at_least(dve, y_out[r % 2], 16 * (m // 2))
                        else:
                            dve.wait_ge(y_out[r % 2], (m - r % 2) * 8)
                    at_least(dve, S["expv"], m * T + t + 1)
                else:
                    dve.wait_ge(S["acc"], m * 16 + t * 4 + e)
                a = acc[:, r % 2, tile_of(t)]
                v.scalar_tensor_tensor(out=a, in0=unit_bank(2 * t)[:, e * P:(e + 1) * P],
                                       scalar=gate[:, r % 2, t, e:e + 1],
                                       in1=x2[:, r, tile_of(t)] if e == 0 else a,
                                       op0=ALU.mult, op1=ALU.add).then_inc(S["acc"], 1)

            def split1(n, g):
                if runs(n, "proj"):
                    at_least(dve, S["hi1"], n - LAG["proj"] + 1)
                    v.tensor_tensor(x1l[:, :], t0[:, :], x1h[:, :], ALU.subtract).then_inc(S["lo1"], 1)

            def split2(n, g):
                if runs(n, "route"):
                    m, r = n - LAG["route"], (g - LAG["route"]) % 4
                    at_least(dve, S["hi2"], m + 1)
                    v.tensor_tensor(x2l[0:P - 1, r, :], t1[0:P - 1, :], x2h[0:P - 1, r, :], ALU.subtract).then_inc(S["lo2"], 1)

            def max_q(n, g):
                if runs(n, "q"):
                    at_least(dve, S["kv"], n - LAG["q"] + 1)
                    v.tensor_reduce(qmax[:, :].rearrange("p (t h) -> p t h", t=T),
                                    q_ps.rearrange("p t (h k) -> p t h k", k=DH), op=ALU.max, axis=AX_X).then_inc(S["qmax"], 1)

            def subtract_qmax(n, g):
                if runs(n, "q"):
                    m, r = n - LAG["q"], (g - LAG["q"]) % BLOCK
                    dve.wait_ge(S["qmax"], m + 1)
                    at_least(dve, S["qn"], m - BLOCK + 1)
                    v.tensor_tensor(qe[:, r, :].rearrange("p (t h k) -> p t h k", t=T, k=DH),
                                    q_ps.rearrange("p t (h k) -> p t h k", k=DH),
                                    qmax[:, :].rearrange("p (t h) -> p t h", t=T).unsqueeze(3).to_broadcast([P, T, HEADS, DH]),
                                    ALU.subtract).then_inc(S["qsub"], 1)

            def max_k(n, b, g):
                if runs(n, "kmax"):
                    m, r = n - LAG["kmax"], (g - LAG["kmax"]) % BLOCK
                    km, k3 = kmax[:, :].rearrange("p (t c) -> p t c", t=T), kv[:, r, :, 0:P]
                    at_least(dve, S["kv"], m + 1)
                    if r % G == 0:
                        v.tensor_copy(km, k3).then_inc(S["kmax"], 1)
                    else:
                        dve.wait_ge(S["kmax"], m)
                        v.tensor_tensor(km, km, k3, ALU.max).then_inc(S["kmax"], 1)

            def reduce_kmax(n, b, g):
                done = batch_end(n - 1, b, g - 1, LAG["kmax"])
                if done is not None:
                    dve.wait_ge(S["kmax"], done * G)
                    at_least(dve, S["kturn"], done - 1)
                    v.tensor_reduce(kred[:, :], kmax[:, :].rearrange("p (t c) -> p c t", t=T), op=ALU.max, axis=AX_X)\
                        .then_inc(S["kred"], 1)

            def column_kmax(n, b, g):
                done = batch_end(n - 1, b, g - 1, LAG["kmax"])
                if done is not None:
                    dve.wait_ge(S["kturn"], done)
                    v.tensor_reduce(kcol[:, :], t0[:, 0:P], op=ALU.max, axis=AX_X).then_inc(S["kcol"], 1)

            def diagonal_kmax(n, b, g):
                done = batch_end(n - 1, b, g - 1, LAG["kmax"])
                if done is not None:
                    dve.wait_ge(S["kcol"], done)
                    v.tensor_scalar(kdiag[:, :], ident[:, :], kcol[:, 0:1], None, ALU.mult).then_inc(S["kdiag"], 1)

            def sum_q(n, g):
                if runs(n, "qsum"):
                    m, r = n - LAG["qsum"], (g - LAG["qsum"]) % BLOCK
                    at_least(dve, S["qexp"], m + 1)
                    v.tensor_reduce(qsum[:, :], qe[:, r, :].rearrange("p (h k) -> p h k", k=DH), op=ALU.add, axis=AX_X)\
                        .then_inc(S["qsum"], 1)

            def invert_qsum(n, g):
                if runs(n, "qsum"):
                    m, r = n - LAG["qsum"], (g - LAG["qsum"]) % BLOCK
                    dve.wait_ge(S["qsum"], m + 1)
                    v.reciprocal(qr[:, r, :], qsum[:, :]).then_inc(S["qr"], 1)

            def sum_context(n, g):
                if runs(n, "ctx"):
                    m, r = n - LAG["ctx"], (g - LAG["ctx"]) % G
                    at_least(dve, S["ctx"], m + 1)
                    if r == 0:
                        at_least(dve, S["cn"], (m + 1) // G if isinstance(m, int) else 1)
                        v.tensor_copy(csum[:, :], ctx_ps).then_inc(S["csum"], 1)
                    else:
                        dve.wait_ge(S["csum"], m)
                        v.tensor_tensor(csum[:, :], ctx_ps, csum[:, :], ALU.add).then_inc(S["csum"], 1)

            def invert_ksum(n, b, g):
                done = batch_end(n, b, g, LAG["ctx"])
                if done is not None:
                    dve.wait_ge(S["csum"], done * G)
                    v.reciprocal(rksum[:, :], csum[:, P:P + 1]).then_inc(S["rk"], 1)

            def normalise_context(n, b, g):
                done = batch_end(n, b, g, LAG["ctx"])
                if done is not None:
                    dve.wait_ge(S["rk"], done)
                    at_least(dve, S["cturn"], done - 1)
                    v.scalar_tensor_tensor(out=cn[:, :], in0=csum[:, 0:P], scalar=rksum[:, 0:1], in1=head_mask[:, :],
                                           op0=ALU.mult, op1=ALU.mult).then_inc(S["cn"], 1)

            def finish_mix(n, b, g):
                done = batch_end(n - 1, b, g - 1, LAG["ctx"])
                if done is not None:
                    dve.wait_ge(S["mixp"], done)
                    at_least(dve, S["o"], upto(n - 1 - LAG["out"]))
                    v.tensor_tensor(mix[:, :], t0[:, 0:P], bo[:, :], ALU.add).then_inc(S["mix"], 1)

            def gates_logit(n, g):
                if runs(n, "route"):
                    m = n - LAG["route"]
                    at_least(dve, S["rout"], m + 1)
                    at_least(dve, S["topi"], m)
                    v.tensor_copy(logit[:, :, :], t1[:, 0:T * E].rearrange("p (t e) -> p t e", t=T)).then_inc(S["logit"], 1)

            def gates_top(n, g):
                if runs(n, "route"):
                    dve.wait_ge(S["logit"], n - LAG["route"] + 1)
                    step_on(dve, S["dve_go"])
                    for t in range(T):
                        last = v.max(top[:, t, :], logit[:, t, :])
                    last.then_inc(S["top"], 1)

            def gates_gap(n, g):
                if runs(n, "route"):
                    m = n - LAG["route"]
                    dve.wait_ge(S["top"], m + 1)
                    at_least(dve, S["e2"], m)
                    v.tensor_tensor(gap[:, :], top[:, :, 1], top[:, :, 0], ALU.subtract).then_inc(S["gap"], 1)
                    for t in range(T):
                        last = v.max_index(top_i[:, t, :], top[:, t, :], logit[:, t, :])
                    last.then_inc(S["topi"], 1)

            def gates_onehot(n, g, k):
                if runs(n, "gates"):
                    m = n - LAG["gates"]
                    if k == 0:
                        dve.wait_ge(S["topi"], m + 1)
                        at_least(dve, S["gate"], m)
                    last = v.tensor_tensor((oh1, oh2)[k][:, :, :], expert_no[:, :, :],
                                           top_i[:, :, k:k + 1].to_broadcast([P, T, E]), ALU.is_equal)
                    if k == 1:
                        last.then_inc(S["oh"], 1)

            def gates_sum(n, g):
                if runs(n, "gates"):
                    at_least(dve, S["e2"], n - LAG["gates"] + 1)
                    v.tensor_scalar(e2p[:, :], e2[:, :], 1.0, None, ALU.add).then_inc(S["e2p"], 1)

            def gates_recip(n, g):
                if runs(n, "gates"):
                    dve.wait_ge(S["e2p"], n - LAG["gates"] + 1)
                    v.reciprocal(r2[:, :], e2p[:, :]).then_inc(S["r2"], 1)

            def gates_first(n, g):
                if runs(n, "gates"):
                    m = n - LAG["gates"]
                    dve.wait_ge(S["r2"], m + 1)
                    at_least(dve, S["gb"], m)
                    v.tensor_scalar(g1[:, :], r2[:, :], sigma[:, 1:2], None, ALU.mult).then_inc(S["g1"], 1)

            def gates_second(n, g):
                if runs(n, "gates"):
                    m = n - LAG["gates"]
                    dve.wait_ge(S["g1"], m + 1)
                    v.tensor_tensor(g2[:, :], g1[:, :], e2[:, :], ALU.mult).then_inc(S["g2"], 1)

            def slot(n, b, g):
                finish_mix(n, b, g)
                stats1(n, b, g, 0)
                weigh(n, g, 0, 0)
                stats1(n, b, g, 1)
                gates_onehot(n, g, 0)
                weigh(n, g, 0, 1)
                stats1(n, b, g, 2)
                gates_onehot(n, g, 1)
                weigh(n, g, 0, 2)
                stats1(n, b, g, 3)
                gates_sum(n, g)
                weigh(n, g, 0, 3)
                reduce_kmax(n, b, g)
                for t in range(T):
                    stats3(n, g, t)
                gates_recip(n, g)
                split1(n, g)
                column_kmax(n, b, g)
                gates_first(n, g)
                stats2(n, g, 0)
                diagonal_kmax(n, b, g)
                stats2(n, g, 1)
                gates_second(n, g)
                stats2(n, g, 2)
                stats2(n, g, 3)
                weigh(n, g, 1, 0)
                moments_parts(n)
                weigh(n, g, 1, 1)
                moments_squares(n)
                weigh(n, g, 1, 2)
                moments_var(n)
                weigh(n, g, 1, 3)
                split2(n, g)
                sum_q(n, g)
                weigh(n, g, 2, 0)
                invert_qsum(n, g)
                moments_mean(n)
                weigh(n, g, 2, 1)
                sum_context(n, g)
                weigh(n, g, 2, 2)
                invert_ksum(n, b, g)
                gates_logit(n, g)
                weigh(n, g, 2, 3)
                normalise_context(n, b, g)
                gates_top(n, g)
                max_q(n, g)
                weigh(n, g, 3, 0)
                gates_gap(n, g)
                subtract_qmax(n, g)
                weigh(n, g, 3, 1)
                max_k(n, b, g)
                weigh(n, g, 3, 2)
                weigh(n, g, 3, 3)

            all_slots(dve, slot)


_INS = ["x", "L0_conv_w_qkv", "L0_conv_w_out", "L0_conv_b_out", "L0_conv_ln_scale",
        "L0_ffn_router_w", "L0_ffn_router_b", "L0_ffn_expert_w", "L0_ffn_expert_b"]


def kernel(**inputs):
    import numpy as _np
    import concourse.bacc as _bacc
    from concourse import mybir as _mybir
    from concourse.bass_utils import run_bass_kernel_spmd as _run

    nc = _bacc.Bacc("TRN2", target_bir_lowering=False, num_devices=1)
    arrays, args = {}, []
    for name in _INS:
        a = _np.ascontiguousarray(inputs[name])
        arrays[f"in_{name}"] = a
        args.append(nc.dram_tensor(f"in_{name}", a.shape, _mybir.dt.from_np(a.dtype), kind="ExternalInput").ap())
    args.append(nc.dram_tensor("out_0", inputs["x"].shape, F32, kind="ExternalOutput").ap())
    metaformer_kernel(nc, *args)
    r = _run(nc, [arrays], core_ids=[0])
    return r.results[0]["out_0"]
```

```python
from contextlib import ExitStack

import concourse.bass as bass
from concourse import mybir

F32, F16, U32, I32 = mybir.dt.float32, mybir.dt.float16, mybir.dt.uint32, mybir.dt.int32
ALU = mybir.AluOpType
ACT = mybir.ActivationFunctionType
AX_X = mybir.AxisListType.X
R_MAX = bass.bass_isa.ReduceOp.max

P = 128
HEADS, DH = 4, 32
E = 8
T = 4
G = 8
BLOCK = 16
BODY = 2 * BLOCK
W3 = 3 * P
CX = P + 1
HALF = E // 2
ACC = (T - 1) * HALF
XS = 256.0
WS = 1024.0
LN_XS = 5.545177444479562

LAG = dict(
    st1=0, xn1=1, x1t=1, hi1=1, lo1=1, qv=1, kt=1,
    vc=1, qmax=2, qsub=2, qexp=2, qsum=3, qr=4,
    kmax=1, nk=1, kexp=2, ket=2, ke=2, alpha=2,
    ctx=2, csum=2,
    rk=2, cn=2, cturn=2, cnt=2, mixp=3, mix=3,
    qn=8, qt=10, qtc=9, o=10,
    st3=10, res=10, x2=11,
    st2=11, xn2=12, xn2p=12, x2t=12, hi2=12, lo2=12, rout=12,
    logit=12, top=12, topi=12, oh1=13, oh2=13, e2=12, e2p=13, r2=13, g1=13, g2=13, gb=13, gate=14,
    experts=14, weigh=14, prod=14, prodb=14, extra=15, extra2=15, extra3=15, pairs=15, ysum=15, y=15, store=18,
)

PREPARE = dict(fold=1, largest=3, split=4, use=7)


def at_least(eng, sem, value):
    if isinstance(value, int) and value < 1:
        return
    eng.wait_ge(sem, value)


def step_on(eng, going):
    eng.sem_inc(going, 1)


def metaformer_kernel(nc, x, w_qkv, w_out, b_out, ln_scale, router_w, router_b, expert_w, expert_b, out):
    B = x.shape[0]
    N = x.shape[1] * x.shape[2]
    M = B * G
    assert N == G * T * P
    x_v = x.rearrange("b h w c -> (b h w) c").rearrange("(m p t) c -> m p (t c)", m=M, p=P)
    out_v = out.rearrange("b h w c -> (b h w) c").rearrange("(m p t) c -> m p (t c)", m=M, p=P)
    SLOTS = M + max(LAG.values()) + 1
    FILL = BODY
    LOOPS = max(0, M - FILL) // BODY

    ctx = ExitStack()
    with ctx:
        def sb(name, shape, dt=F32):
            return ctx.enter_context(nc.sbuf_tensor(name, shape, dt))

        def ps(name, shape):
            return ctx.enter_context(nc.psum_tensor(name, shape, F32))

        def sem(name):
            return ctx.enter_context(nc.semaphore(name))

        ident = sb("ident", [P, P])
        ones = sb("ones", [P, P])
        zero_col, ln_xs = sb("zero_col", [P, 1]), sb("ln_xs", [P, 1])
        eps = sb("eps", [P, 3 * T])
        expert_no = sb("expert_no", [P, T, E])
        expert_no_i = sb("expert_no_i", [P, T, E], I32)
        head_mask = sb("head_mask", [P, P])
        wq = sb("wq", [P, W3]); wq_h = sb("wq_h", [P, W3], F16); wq_l = sb("wq_l", [P, W3], F16)
        we_h = sb("we_h", [P, E * P], F16); we_l = sb("we_l", [P, E * P], F16)
        wr = sb("wr", [P, E]); wr_h = sb("wr_h", [P, E], F16); wr_l = sb("wr_l", [P, E], F16)
        wr_last = sb("wr_last", [P, E])
        wo, bo, ln_s = sb("wo", [P, 2 * P]), sb("bo", [P, 2 * P]), sb("ln_s", [P, P])
        wmax, wgmax, wscale = sb("wmax", [P, 4]), sb("wgmax", [P, 4]), sb("wscale", [P, 4])
        sigma = sb("sigma", [P, 4])
        mean_w = sb("mean_w", [P, 2])

        xa = sb("xa", [P, 4, T * P])
        xc = sb("xc", [P, 4, T * P])
        st = sb("st", [P, 3 * T, 6])
        sd, sm, s1, s2, sq, var, lnv, rs, nmr = (sb(n, [P, 3 * T]) for n in "sd sm s1 s2 sq var lnv rs nmr".split())
        xn1 = sb("xn1", [P, T * P])
        x1h, x1l = sb("x1h", [P, T * P], F16), sb("x1l", [P, T * P], F16)
        qe = sb("qe", [P, BLOCK, T * P])
        qr = sb("qr", [P, BLOCK, T * HEADS])
        vone = sb("vone", [P, 4, T, CX])
        kmax, bound, shrink = sb("kmax", [P, 1]), sb("bound", [P, 2]), sb("shrink", [P, 2])
        ket = sb("ket", [P, 2, T * P])
        ke = sb("ke", [P, 2, T * P])
        csum = sb("csum", [P, P + 1])
        rksum = sb("rksum", [P, 1])
        cn, cnt, mix = sb("cn", [P, P]), sb("cnt", [P, P]), sb("mix", [P, 2 * P])
        qn, qt = sb("qn", [P, 2, T * P]), sb("qt", [P, T * P])
        res = sb("res", [P, T * P])
        x2 = sb("x2", [P, 8, T * P])
        xn2 = sb("xn2", [P, T * P])
        x2h, x2l = sb("x2h", [P, 4, T * P], F16), sb("x2l", [P, 4, T * P], F16)
        qmax, qsum = sb("qmax", [P, T * HEADS]), sb("qsum", [P, T * HEADS])
        logit = sb("logit", [P, T, E])
        top = sb("top", [P, T, 8]); top_i = sb("top_i", [P, T, 8], U32)
        gap, e2, e2p, r2 = (sb(n, [P, T]) for n in ("gap", "e2", "e2p", "r2"))
        g12, oh12 = sb("g12", [P, 2 * T]), sb("oh12", [P, 2 * T, E])
        g1, g2 = g12[:, 0:T], g12[:, T:2 * T]
        oh1, oh2 = oh12[:, 0:T, :], oh12[:, T:2 * T, :]
        gate = sb("gate", [P, 2, T, E])
        acc = sb("acc", [P, 4, T * P])
        prod = sb("prod", [P, 2, HALF, T * P])
        prod3 = sb("prod3", [P, 2, HALF, P])
        we = prod[:, 0, 0:2, :].rearrange("p a b -> p (a b)")
        we_last = prod[:, 0, 2:4, :].rearrange("p a b -> p (a b)")

        t0 = ps("t0", [P, 512])
        t1 = ps("t1", [P, 512])
        pq = ps("pq", [P, 2 * 512])
        pk = ps("pk", [P, 512])
        px = ps("px", [P, 3 * 512])
        o_ps, os_ps = pq[:, 0:512], pq[:, 512:1024]
        ctx_ps = t0[:, 0:P + 1]

        names = """dve_go pool_go rows wq_in w_in w_cast const maskd qmaxed qall qscaled qsplit folded emaxed eall escaled esplit centred
            st1 st2 st3 sparts squares var lnv rs nmr xn1 x1t hi1 lo1 qv qmax qsub qexp qsum qr
            kt kmax bound shrink kexp ket ke v ctx csum rk cn cturn cnt mixp mix
            qn qt qtc o res x2 xn2
            x2t hi2 lo2 rout logit top gap topi oh1 oh2 e2 e2p r2 g1 g2 gb gate
            expv exps acc prod prod3 pairs ysum pair3 two3 sum3 xn2p y""".split()
        S = {n: sem("s_" + n) for n in names}
        xa_in = [sem(f"s_xa_in{r}") for r in range(4)]
        xc_in = [sem(f"s_xc_in{r}") for r in range(4)]
        y_out = [sem(f"s_y_out{r}") for r in range(4)]

        block = ctx.enter_context(nc.Block())

        def runs(n, step):
            return not isinstance(n, int) or 0 <= n - LAG[step] < M

        def upto(m):
            return min(m + 1, M) if isinstance(m, int) else m + 1

        def all_slots(eng, slot):
            first = FILL if LOOPS else SLOTS
            for n in range(first):
                slot(n, n // BLOCK, n % BLOCK)
            if LOOPS:
                with eng.Fori(FILL // BODY, FILL // BODY + LOOPS) as i:
                    for s in range(BODY):
                        slot(i * BODY + s, i * (BODY // BLOCK) + s // BLOCK, s % BLOCK)
                for n in range(FILL + LOOPS * BODY, SLOTS):
                    slot(n, n // BLOCK, n % BLOCK)

        def batch_end(n, b, g, lag):
            if (g - lag) % G != G - 1 or isinstance(n, int) and not 0 <= n - lag < M:
                return None
            return b * (BLOCK // G) + (g - lag + 1) // G

        def batch_start(n, b, g, lag):
            if (g - lag) % G != 0 or isinstance(n, int) and not 0 <= n - lag < M:
                return None
            return b * (BLOCK // G) + (g - lag) // G

        def stores_before(m, r):
            return (m - r % 4) * 4

        def tile_of(t):
            return slice(t * P, (t + 1) * P)

        q_ps = pq[:, :].rearrange("p (t c) -> p t c", t=T)[:, :, 0:P]
        v_ps = pq[:, :].rearrange("p (t c) -> p t c", t=T)[:, :, P:2 * P]

        def unit_bank(u):
            return px[:, (u % 3) * 512:(u % 3 + 1) * 512]

        @block.sync
        def _(sp):
            for col, of in ((0, 0), (P, 2 * P), (2 * P, P)):
                sp.dma_start(wq[:, col:col + P], w_qkv[:, of:of + P]).then_inc(S["wq_in"], 16)
            sp.dma_start(xa[:, 0, :], x_v[0]).then_inc(xa_in[0], 16)
            sp.dma_start(we.rearrange("c (e n) -> c e n", e=E), expert_w.rearrange("e c n -> c e n")).then_inc(S["w_in"], 16)
            sp.dma_start(wr[:, :], router_w).then_inc(S["w_in"], 16)
            sp.dma_start(we_last.rearrange("c (e n) -> c e n", e=E),
                         expert_w[:, P - 1, :].partition_broadcast(P)).then_inc(S["w_in"], 16)
            sp.dma_start(wr_last[:, :], router_w[P - 1, :].partition_broadcast(P)).then_inc(S["w_in"], 16)
            sp.dma_start(wo[:, 0:P], w_out).then_inc(S["w_in"], 16)
            sp.dma_start(bo[:, 0:P], b_out.partition_broadcast(P)).then_inc(S["w_in"], 16)
            sp.dma_start(ln_s[:, :], ln_scale.partition_broadcast(P)).then_inc(S["w_in"], 16)
            sp.wait_ge(S["folded"], 2)
            sp.dma_start(we[P - 1:P, :], expert_b.rearrange("e n -> (e n)").unsqueeze(0)).then_inc(S["w_cast"], 16)
            sp.dma_start(wr[P - 1:P, :], router_b.unsqueeze(0)).then_inc(S["w_cast"], 16)

            def slot(n, b, g):
                if runs(n, "st1"):
                    at_least(sp, S["xn1"], n - 3)
                    if not (isinstance(n, int) and n == 0):
                        sp.dma_start(xa[:, g % 4, :], x_v[n]).then_inc(xa_in[g % 4], 16)
                if runs(n + 2, "x2"):
                    m, r = n + 2 - LAG["x2"], (g + 2 - LAG["x2"]) % 4
                    at_least(sp, S["x2"], m - 3)
                    sp.dma_start(xc[:, r, :], x_v[m]).then_inc(xc_in[r], 16)
                if runs(n, "store"):
                    m, r = n - LAG["store"], (g - LAG["store"]) % 4
                    at_least(sp, S["y"], m + 1)
                    sp.dma_start(out_v[m], acc[:, r, :]).then_inc(y_out[r], 16)

            all_slots(sp, slot)
            for r in range(4):
                sp.wait_ge(y_out[r], 16 * (M // 4))

        @block.tensor
        def _(pe):
            mm = nc.tensor.matmul
            pe.wait_ge(S["const"], 4)
            pe.wait_ge(S["rows"], 3)
            pe.wait_ge(S["qsplit"], 2)

            def turn(dst, src, t):
                return nc.tensor.transpose(dst[:, tile_of(t)], src[:, tile_of(t)], ident[:, :])

            def experts(n, g, t, half):
                if not runs(n, "experts"):
                    return
                m, r = n - LAG["experts"], (g - LAG["experts"]) % 4
                hi, lo = x2h[:, r, tile_of(t)], x2l[:, r, tile_of(t)]
                u = 2 * t + half
                had, of = (u - 3, m) if u >= 3 else ((6, 7, 5)[u], m - 1)
                if had == 6:
                    at_least(pe, S["prod3"], of + 1)
                elif had % 2 == 0:
                    at_least(pe, S["acc"], of * ACC + (had // 2) * HALF + HALF)
                else:
                    at_least(pe, S["prod"], of * 4 + had // 2 + 1)
                w = slice(half * 512, half * 512 + 512)
                mm(unit_bank(u), hi, we_h[:, w], start=True, stop=False)
                mm(unit_bank(u), hi, we_l[:, w], start=False, stop=False)
                mm(unit_bank(u), lo, we_h[:, w], start=False, stop=True).then_inc(S["exps" if half else "expv"], 1)

            def turn_x1(n, b, g):
                if runs(n, "x1t"):
                    m = n - LAG["x1t"]
                    at_least(pe, S["xn1"], m + 1)
                    done = batch_end(n, b, g, LAG["mixp"])
                    if done is not None:
                        pe.wait_ge(S["mix"], done)
                    done = batch_end(n - 1, b, g - 1, LAG["cturn"])
                    if done is not None:
                        pe.wait_ge(S["cnt"], done)
                    at_least(pe, S["csum"], upto(n - 1 - LAG["ctx"]))
                    for t in range(T):
                        last = turn(t0, xn1, t)
                    last.then_inc(S["x1t"], 1)

            def project_qv(n, g):
                if runs(n, "qv"):
                    m = n - LAG["qv"]
                    at_least(pe, S["hi1"], m + 1)
                    at_least(pe, S["lo1"], m + 1)
                    at_least(pe, S["st3"], upto(n - LAG["o"]))
                    at_least(pe, S["res"], upto(n - LAG["o"]))
                    for t in range(T):
                        hi, lo, at = x1h[:, tile_of(t)], x1l[:, tile_of(t)], slice(t * 2 * P, (t + 1) * 2 * P)
                        mm(pq[:, at], hi, wq_h[:, 0:2 * P], start=True, stop=False)
                        mm(pq[:, at], hi, wq_l[:, 0:2 * P], start=False, stop=False)
                        last = mm(pq[:, at], lo, wq_h[:, 0:2 * P], start=False, stop=True)
                    last.then_inc(S["qv"], 1)

            def project_k(n, g):
                if runs(n, "kt"):
                    m = n - LAG["kt"]
                    at_least(pe, S["hi1"], m + 1)
                    at_least(pe, S["lo1"], m + 1)
                    at_least(pe, S["kexp"], m)
                    mm(pk[:, :], wq_h[:, 2 * P:W3], x1h[:, :], start=True, stop=False)
                    mm(pk[:, :], wq_l[:, 2 * P:W3], x1h[:, :], start=False, stop=False)
                    mm(pk[:, :], wq_h[:, 2 * P:W3], x1l[:, :], start=False, stop=True).then_inc(S["kt"], 1)

            def turn_k(n, b, g):
                if runs(n, "ket"):
                    m = n - LAG["ket"]
                    at_least(pe, S["kexp"], m + 1)
                    at_least(pe, S["lo1"], upto(n - LAG["x1t"]))
                    for t in range(T):
                        last = turn(t0, ket[:, (g - LAG["ket"]) % 2, :], t)
                    last.then_inc(S["ket"], 1)

            def turn_q(n, g):
                if runs(n, "qt"):
                    m = n - LAG["qt"]
                    at_least(pe, S["qn"], m + 1)
                    at_least(pe, S["logit"], upto(n - 1 - LAG["rout"]))
                    for t in range(T):
                        last = turn(t1, qn[:, (g - LAG["qt"]) % 2, :], t)
                    last.then_inc(S["qt"], 1)

            def attend(n, b, g):
                if runs(n, "o"):
                    m = n - LAG["o"]
                    before = batch_start(n, b, g, LAG["o"])
                    if before is not None:
                        pe.wait_ge(S["mix"], before + 1)
                    at_least(pe, S["qtc"], m + 1)
                    at_least(pe, S["v"], upto(n - 1 - LAG["qv"]))
                    at_least(pe, S["qsub"], upto(n - 1 - LAG["qv"]))
                    for t in range(T):
                        mm(o_ps[:, tile_of(t)], qt[:, tile_of(t)], mix[:, 0:P], start=True, stop=True)
                        last = mm(os_ps[:, tile_of(t)], qt[:, tile_of(t)], mix[:, P:2 * P], start=True, stop=True)
                    last.then_inc(S["o"], 1)

            def turn_x2(n, g):
                if runs(n, "x2t"):
                    m = n - LAG["x2t"]
                    at_least(pe, S["xn2"], m + 1)
                    at_least(pe, S["xn2p"], m + 1)
                    at_least(pe, S["qtc"], upto(n - LAG["qt"]))
                    for t in range(T):
                        last = turn(t1, xn2, t)
                    last.then_inc(S["x2t"], 1)

            def route(n, g):
                if runs(n, "rout"):
                    m, r = n - LAG["rout"], (g - LAG["rout"]) % 4
                    at_least(pe, S["hi2"], m + 1)
                    at_least(pe, S["lo2"], m + 1)
                    for t in range(T):
                        hi, lo = x2h[:, r, tile_of(t)], x2l[:, r, tile_of(t)]
                        o = t1[:, t * E:(t + 1) * E]
                        mm(o, hi, wr_h[:, :], start=True, stop=False)
                        mm(o, hi, wr_l[:, :], start=False, stop=False)
                        last = mm(o, lo, wr_h[:, :], start=False, stop=True)
                    last.then_inc(S["rout"], 1)

            def add_context(n, b, g):
                if runs(n, "ctx"):
                    m, r = n - LAG["ctx"], (g - LAG["ctx"]) % 4
                    at_least(pe, S["ke"], m + 1)
                    at_least(pe, S["v"], m + 1)
                    for t in range(T):
                        last = mm(ctx_ps, ke[:, r % 2, tile_of(t)], vone[:, r, t, :], start=(t == 0), stop=(t == T - 1))
                    last.then_inc(S["ctx"], 1)

            def turn_context(n, b, g):
                done = batch_end(n, b, g, LAG["cturn"])
                if done is not None:
                    pe.wait_ge(S["cn"], done)
                    at_least(pe, S["csum"], upto(n - LAG["ctx"]))
                    nc.tensor.transpose(t0[:, 0:P], cn[:, :], ident[:, :]).then_inc(S["cturn"], 1)

            def mix_context(n, b, g):
                done = batch_end(n, b, g, LAG["mixp"])
                if done is not None:
                    pe.wait_ge(S["cnt"], done)
                    at_least(pe, S["csum"], upto(n - 1 - LAG["ctx"]))
                    mm(t0[:, 0:2 * P], cnt[:, :], wo[:, :], start=True, stop=True).then_inc(S["mixp"], 1)

            def slot(n, b, g):
                if isinstance(n, int) and n == PREPARE["use"]:
                    pe.wait_ge(S["centred"], 7)
                    pe.wait_ge(S["esplit"], 4)
                mix_context(n, b, g)
                experts(n, g, 0, 0)
                turn_q(n, g)
                turn_x1(n, b, g)
                experts(n, g, 0, 1)
                experts(n, g, 1, 0)
                attend(n, b, g)
                turn_k(n, b, g)
                experts(n, g, 1, 1)
                turn_x2(n, g)
                experts(n, g, 2, 0)
                add_context(n, b, g)
                project_k(n, g)
                experts(n, g, 2, 1)
                experts(n, g, 3, 0)
                route(n, g)
                turn_context(n, b, g)
                project_qv(n, g)
                experts(n, g, 3, 1)

            all_slots(pe, slot)

        @block.scalar
        def _(act):
            af = nc.scalar.activation
            nc.scalar.preload_act_table_set("natural_log_exp_and_others")
            act.wait_ge(S["const"], 4)
            act.wait_ge(S["rows"], 3)
            act.wait_ge(S["qsplit"], 2)

            def products(n, g, t):
                if not runs(n, "prod"):
                    return
                m, r = n - LAG["prod"], (g - LAG["prod"]) % 2
                at_least(act, S["gate"], m + 1)
                if t == 0:
                    at_least(act, S["y"], m - 1)
                at_least(act, S["exps"], m * T + t + 1)
                for e in range(HALF):
                    last = af(prod[:, r, e, tile_of(t)], unit_bank(2 * t + 1)[:, e * P:(e + 1) * P], ACT.Copy,
                              scale=gate[:, r, t, HALF + e:HALF + e + 1])
                last.then_inc(S["prod"], 1)

            def split1(n, g):
                if runs(n, "hi1"):
                    m = n - LAG["hi1"]
                    at_least(act, S["x1t"], m + 1)
                    at_least(act, S["qv"], m)
                    at_least(act, S["kt"], m)
                    nc.scalar.copy(x1h[:, :], t0[:, :]).then_inc(S["hi1"], 1)

            def products_last(n, g):
                if runs(n, "prodb"):
                    m, r = n - LAG["prodb"], (g - LAG["prodb"]) % 2
                    at_least(act, S["gate"], m + 1)
                    at_least(act, S["expv"], m * T + T)
                    at_least(act, S["sum3"], m - 1)
                    for e in range(HALF):
                        last = af(prod3[:, r, e, :], unit_bank(2 * T - 2)[:, e * P:(e + 1) * P], ACT.Copy,
                                  scale=gate[:, r, T - 1, e:e + 1])
                    last.then_inc(S["prod3"], 1)

            def copy_qt(n, g):
                if runs(n, "qtc"):
                    m = n - LAG["qtc"]
                    at_least(act, S["qt"], m + 1)
                    at_least(act, S["o"], m)
                    nc.scalar.copy(qt[:, :], t1[:, :]).then_inc(S["qtc"], 1)

            def split2(n, g):
                if runs(n, "hi2"):
                    m, r = n - LAG["hi2"], (g - LAG["hi2"]) % 4
                    at_least(act, S["x2t"], m + 1)
                    at_least(act, S["expv"], (m - 3) * T)
                    at_least(act, S["exps"], (m - 3) * T)
                    at_least(act, S["rout"], m - 3)
                    nc.scalar.copy(x2h[0:P - 1, r, :], t1[0:P - 1, :]).then_inc(S["hi2"], 1)

            def rstd_log(n):
                at_least(act, S["var"], n + 1)
                af(lnv[:, :], var[:, :], ACT.Ln, bias=zero_col[:, 0:1]).then_inc(S["lnv"], 1)

            def rstd_exp(n):
                at_least(act, S["lnv"], n + 1)
                at_least(act, S["xn1"], upto(n - 1 - LAG["st1"]))
                at_least(act, S["xn2"], upto(n - 1 - LAG["st2"]))
                at_least(act, S["xn2p"], upto(n - 1 - LAG["st2"]))
                at_least(act, S["res"], upto(n - 1 - LAG["st3"]))
                at_least(act, S["nmr"], n)
                af(rs[:, :], lnv[:, :], ACT.Exp, bias=ln_xs[:, 0:1], scale=-0.5).then_inc(S["rs"], 1)

            def scale_att(n, g):
                if runs(n, "res"):
                    m = n - LAG["res"]
                    at_least(act, S["rs"], m + LAG["st3"] + 1)
                    at_least(act, S["o"], m + 1)
                    at_least(act, S["x2"], m)
                    for t in range(T):
                        last = af(res[:, tile_of(t)], os_ps[:, tile_of(t)], ACT.Copy, scale=rs[:, T + t:T + t + 1])
                    last.then_inc(S["res"], 1)

            def normalise_x2(n, g):
                if runs(n, "xn2"):
                    m, r = n - LAG["xn2"], (g - LAG["xn2"]) % 8
                    at_least(act, S["nmr"], m + LAG["st2"] + 1)
                    at_least(act, S["x2t"], m)
                    for t in range(T // 2):
                        last = af(xn2[:, tile_of(t)], x2[:, r, tile_of(t)], ACT.Identity,
                                  bias=nmr[:, 2 * T + t:2 * T + t + 1], scale=rs[:, 2 * T + t:2 * T + t + 1])
                    last.then_inc(S["xn2"], 1)

            def copy_v(n, g):
                if runs(n, "vc"):
                    m, r = n - LAG["vc"], (g - LAG["vc"]) % 4
                    at_least(act, S["qv"], m + 1)
                    at_least(act, S["ctx"], m - 3)
                    nc.scalar.copy(vone[:, r, :, 0:P], v_ps).then_inc(S["v"], 1)

            def copy_k(n, g):
                if runs(n, "ke"):
                    m = n - LAG["ke"]
                    at_least(act, S["ket"], m + 1)
                    at_least(act, S["ctx"], m - 1)
                    nc.scalar.copy(ke[:, (g - LAG["ke"]) % 2, :], t0[:, :]).then_inc(S["ke"], 1)

            def exp_q(n, g):
                if runs(n, "qexp"):
                    m, r = n - LAG["qexp"], (g - LAG["qexp"]) % BLOCK
                    at_least(act, S["qsub"], m + 1)
                    af(qe[:, r, :], qe[:, r, :], ACT.Exp, bias=zero_col[:, 0:1], scale=sigma[:, 0:1]).then_inc(S["qexp"], 1)

            def exp_k(n, g):
                if runs(n, "kexp"):
                    m, r = n - LAG["kexp"], (g - LAG["kexp"]) % 2
                    at_least(act, S["bound"], m + 1)
                    at_least(act, S["ket"], m - 1)
                    af(ket[:, r, :], pk[:, :], ACT.Exp, bias=bound[:, r:r + 1], scale=sigma[:, 0:1]).then_inc(S["kexp"], 1)

            def exp_shrink(n, g):
                if runs(n, "alpha"):
                    m, r = n - LAG["alpha"], (g - LAG["alpha"]) % G
                    at_least(act, S["bound"], m + 1)
                    at_least(act, S["csum"], m - 1)
                    new, old = r % 2, (r - 1) % 2 if r else r % 2
                    af(shrink[:, new:new + 1], bound[:, old:old + 1], ACT.Exp, bias=bound[:, new:new + 1], scale=-1.0)\
                        .then_inc(S["shrink"], 1)

            def exp_gap(n, g):
                if runs(n, "e2"):
                    m = n - LAG["e2"]
                    at_least(act, S["gap"], m + 1)
                    at_least(act, S["g2"], m)
                    af(e2[:, :], gap[:, :], ACT.Exp, bias=zero_col[:, 0:1], scale=sigma[:, 2:3]).then_inc(S["e2"], 1)

            def copy_context(n, b, g):
                done = batch_end(n, b, g, LAG["cnt"])
                if done is not None:
                    act.wait_ge(S["cturn"], done)
                    at_least(act, S["mixp"], done - 1)
                    nc.scalar.copy(cnt[:, :], t0[:, 0:P]).then_inc(S["cnt"], 1)

            def slot(n, b, g):
                if isinstance(n, int) and n == PREPARE["use"]:
                    act.wait_ge(S["esplit"], 4)
                split1(n, g)
                exp_k(n, g)
                normalise_x2(n, g)
                products(n, g, 0)
                exp_q(n, g)
                copy_k(n, g)
                products(n, g, 1)
                exp_shrink(n, g)
                rstd_log(n)
                split2(n, g)
                rstd_exp(n)
                scale_att(n, g)
                products(n, g, 2)
                copy_context(n, b, g)
                products_last(n, g)
                copy_v(n, g)
                products(n, g, 3)
                exp_gap(n, g)
                copy_qt(n, g)

            all_slots(act, slot)

        @block.gpsimd
        def _(pool):
            gp = nc.gpsimd
            gp.memset(ident[:, :], 0.0)
            gp.memset(ones[:, :], 1.0)
            gp.memset(zero_col[:, :], 0.0)
            gp.memset(eps[:, 0:T], 1e-6)
            gp.memset(eps[:, T:3 * T], 1e-5)
            gp.memset(ln_xs[:, :], LN_XS)
            gp.memset(vone[:, :, :, P:CX], 1.0)
            gp.iota(expert_no_i[:, :, :], pattern=[[0, T], [1, E]], base=0, channel_multiplier=0).then_inc(S["const"], 1)
            pool.wait_ge(S["const"], 1)
            gp.tensor_copy(expert_no[:, :, :], expert_no_i[:, :, :]).then_inc(S["const"], 1)
            gp.affine_select(out=ident[:, :], in_=ident[:, :], compare_op=ALU.not_equal, fill=1.0, base=0,
                             pattern=[[-1, P]], channel_multiplier=1).then_inc(S["const"], 1)
            hm = head_mask[:, :].rearrange("p (h k) -> p h k", h=HEADS)
            gp.affine_select(out=hm, in_=ones[:, :].rearrange("p (h k) -> p h k", h=HEADS), compare_op=ALU.is_ge, fill=0.0,
                             base=0, pattern=[[-DH, HEADS], [0, DH]], channel_multiplier=1).then_inc(S["maskd"], 1)
            pool.wait_ge(S["maskd"], 1)
            gp.affine_select(out=hm, in_=hm, compare_op=ALU.is_ge, fill=0.0,
                             base=DH - 1, pattern=[[DH, HEADS], [0, DH]], channel_multiplier=-1).then_inc(S["const"], 1)
            pool.wait_ge(S["qmaxed"], 1)
            gp.partition_all_reduce(wgmax[:, 0:1], wmax[:, 0:1], P, R_MAX).then_inc(S["qall"], 1)

            def largest_weights():
                pool.wait_ge(S["emaxed"], 2)
                gp.partition_all_reduce(wgmax[:, 1:3], wmax[:, 1:3], P, R_MAX).then_inc(S["eall"], 1)

            def normalise_q(n, g):
                if runs(n, "qn"):
                    m, r = n - LAG["qn"], (g - LAG["qn"]) % BLOCK
                    at_least(pool, S["qr"], m + 1)
                    at_least(pool, S["qt"], m - 1)
                    gp.tensor_tensor(qn[:, r % 2, :].rearrange("p (h k) -> p h k", k=DH),
                                     qe[:, r, :].rearrange("p (h k) -> p h k", k=DH),
                                     qr[:, r, :].unsqueeze(2).to_broadcast([P, T * HEADS, DH]), ALU.mult).then_inc(S["qn"], 1)

            def normalise_x1(n, g):
                if runs(n, "xn1"):
                    m, r = n - LAG["xn1"], (g - LAG["xn1"]) % 4
                    at_least(pool, S["nmr"], m + LAG["st1"] + 1)
                    at_least(pool, S["x1t"], m)
                    step_on(pool, S["pool_go"])
                    for t in range(T):
                        last = gp.tensor_scalar(xn1[:, tile_of(t)], xa[:, r, tile_of(t)],
                                                rs[:, t:t + 1], nmr[:, t:t + 1], ALU.mult, ALU.add)
                    last.then_inc(S["xn1"], 1)

            def residual_sum(n, b, g):
                if runs(n, "x2"):
                    m, r = n - LAG["x2"], g - LAG["x2"]
                    at_least(pool, S["res"], m + 1)
                    pool.wait_ge(xc_in[r % 4], b * (BLOCK // 4 * 16) + (r // 4 + 1) * 16)
                    at_least(pool, S["acc"], (m - 7) * ACC)
                    at_least(pool, S["sum3"], m - 7)
                    gp.tensor_tensor(x2[:, r % 8, :], res[:, :], xc[:, r % 4, :], ALU.add).then_inc(S["x2"], 1)

            def sum_pairs(n, g):
                if runs(n, "pairs"):
                    m, r = n - LAG["pairs"], (g - LAG["pairs"]) % 2
                    at_least(pool, S["prod"], m * T + T)
                    gp.tensor_tensor(prod[:, r, 0:2, :], prod[:, r, 0:2, :], prod[:, r, 2:4, :], ALU.add).then_inc(S["pairs"], 1)

            def sum_products(n, g):
                if runs(n, "ysum"):
                    m, r = n - LAG["ysum"], (g - LAG["ysum"]) % 2
                    at_least(pool, S["pairs"], m + 1)
                    gp.tensor_tensor(prod[:, r, 0, :], prod[:, r, 0, :], prod[:, r, 1, :], ALU.add).then_inc(S["ysum"], 1)

            def sum_last_pairs(n, g):
                if runs(n, "extra"):
                    m, r = n - LAG["extra"], (g - LAG["extra"]) % 2
                    at_least(pool, S["prod3"], m + 1)
                    gp.tensor_tensor(prod3[:, r, 0:2, :], prod3[:, r, 0:2, :], prod3[:, r, 2:4, :], ALU.add).then_inc(S["pair3"], 1)

            def sum_last_two(n, g):
                if runs(n, "extra2"):
                    m, r = n - LAG["extra2"], (g - LAG["extra2"]) % 2
                    at_least(pool, S["pair3"], m + 1)
                    gp.tensor_tensor(prod3[:, r, 0, :], prod3[:, r, 0, :], prod3[:, r, 1, :], ALU.add).then_inc(S["two3"], 1)

            def sum_last(n, g):
                if runs(n, "extra3"):
                    m, r = n - LAG["extra3"], (g - LAG["extra3"]) % 8
                    at_least(pool, S["two3"], m + 1)
                    at_least(pool, S["x2"], m + 1)
                    at_least(pool, y_out[r % 4], stores_before(m, r))
                    gp.tensor_tensor(acc[:, r % 4, tile_of(T - 1)], prod3[:, r % 2, 0, :], x2[:, r, tile_of(T - 1)], ALU.add)\
                        .then_inc(S["sum3"], 1)

            def normalise_x2(n, g):
                if runs(n, "xn2p"):
                    m, r = n - LAG["xn2p"], (g - LAG["xn2p"]) % 8
                    at_least(pool, S["nmr"], m + LAG["st2"] + 1)
                    at_least(pool, S["x2t"], m)
                    step_on(pool, S["pool_go"])
                    for t in range(T // 2, T):
                        last = gp.tensor_scalar(xn2[:, tile_of(t)], x2[:, r, tile_of(t)],
                                                rs[:, 2 * T + t:2 * T + t + 1], nmr[:, 2 * T + t:2 * T + t + 1], ALU.mult, ALU.add)
                    last.then_inc(S["xn2p"], 1)

            def sum_output(n, g):
                if runs(n, "y"):
                    m, r = n - LAG["y"], (g - LAG["y"]) % 4
                    at_least(pool, S["acc"], m * ACC + ACC)
                    at_least(pool, S["sum3"], m + 1)
                    at_least(pool, S["ysum"], m + 1)
                    gp.tensor_tensor(acc[:, r, :], acc[:, r, :], prod[:, r % 2, 0, :], ALU.add).then_inc(S["y"], 1)

            def weigh_onehots(n, g):
                if runs(n, "gb"):
                    m = n - LAG["gb"]
                    at_least(pool, S["oh1"], m + 1)
                    at_least(pool, S["oh2"], m + 1)
                    at_least(pool, S["g2"], m + 1)
                    gp.tensor_tensor(oh12[:, :, :], oh12[:, :, :], g12[:, :].unsqueeze(2).to_broadcast([P, 2 * T, E]), ALU.mult)\
                        .then_inc(S["gb"], 1)

            def sum_gates(n, g):
                if runs(n, "gate"):
                    m, r = n - LAG["gate"], (g - LAG["gate"]) % 2
                    at_least(pool, S["gb"], m + 1)
                    at_least(pool, S["acc"], (m - 1) * ACC)
                    at_least(pool, S["prod3"], m - 1)
                    at_least(pool, S["prod"], (m - 1) * T)
                    gp.tensor_tensor(gate[:, r, :, :], oh1, oh2, ALU.add).then_inc(S["gate"], 1)

            def slot(n, b, g):
                if isinstance(n, int) and n == PREPARE["largest"]:
                    largest_weights()
                normalise_x1(n, g)
                sum_gates(n, g)
                sum_last_pairs(n, g)
                residual_sum(n, b, g)
                sum_pairs(n, g)
                normalise_x2(n, g)
                sum_last_two(n, g)
                sum_products(n, g)
                normalise_q(n, g)
                sum_last(n, g)
                weigh_onehots(n, g)
                sum_output(n, g)

            all_slots(pool, slot)

        @block.vector
        def _(dve):
            v = nc.vector
            v.memset(x2h[96:P, :, :], XS).then_inc(S["rows"], 1)
            v.memset(x2l[96:P, :, :], 0.0).then_inc(S["rows"], 1)
            v.memset(st[:, :, :], 0.0).then_inc(S["rows"], 1)
            dve.wait_ge(S["wq_in"], 16 * 3)
            v.tensor_reduce(wmax[:, 0:1], wq[:, :], op=ALU.max, axis=AX_X, apply_absolute_value=True).then_inc(S["qmaxed"], 1)
            dve.wait_ge(S["qall"], 1)
            v.tensor_scalar(wgmax[:, 0:1], wgmax[:, 0:1], 1e-30, None, ALU.max).then_inc(S["qscaled"], 1)
            dve.wait_ge(S["qscaled"], 1)
            v.reciprocal(wscale[:, 0:1], wgmax[:, 0:1]).then_inc(S["qscaled"], 1)
            v.tensor_scalar(sigma[:, 3:4], wgmax[:, 0:1], -1.0 / (WS * XS), None, ALU.mult)
            v.tensor_scalar(sigma[:, 0:1], wgmax[:, 0:1], 1.0 / (WS * XS), None, ALU.mult).then_inc(S["qscaled"], 1)
            dve.wait_ge(S["qscaled"], 3)
            v.tensor_scalar(wq[:, :], wq[:, :], wscale[:, 0:1], WS, ALU.mult, ALU.mult).then_inc(S["qscaled"], 1)
            dve.wait_ge(S["qscaled"], 4)
            v.tensor_copy(wq_h[:, :], wq[:, :]).then_inc(S["qsplit"], 1)
            dve.wait_ge(S["qsplit"], 1)
            v.tensor_tensor(wq_l[:, :], wq[:, :], wq_h[:, :], ALU.subtract).then_inc(S["qsplit"], 1)
            dve.wait_ge(S["rows"], 3)

            def centre_w_out():
                dve.wait_ge(S["w_in"], 16 * 7)
                v.tensor_reduce(mean_w[:, 0:1], wo[:, 0:P], op=ALU.add, axis=AX_X)
                v.tensor_reduce(mean_w[:, 1:2], bo[:, 0:P], op=ALU.add, axis=AX_X).then_inc(S["centred"], 1)
                dve.wait_ge(S["centred"], 1)
                v.tensor_scalar(mean_w[:, :], mean_w[:, :], 1.0 / P, None, ALU.mult).then_inc(S["centred"], 1)
                dve.wait_ge(S["centred"], 2)
                v.tensor_scalar(wo[:, 0:P], wo[:, 0:P], mean_w[:, 0:1], None, ALU.subtract).then_inc(S["centred"], 1)
                v.tensor_scalar(bo[:, 0:P], bo[:, 0:P], mean_w[:, 1:2], 1.0 / HEADS, ALU.subtract, ALU.mult).then_inc(S["centred"], 1)
                dve.wait_ge(S["centred"], 4)
                for w in (wo, bo):
                    v.scalar_tensor_tensor(out=w[:, P:2 * P], in0=w[:, 0:P], scalar=1.0 / XS, in1=ln_s[:, :],
                                           op0=ALU.mult, op1=ALU.mult).then_inc(S["centred"], 1)
                dve.wait_ge(S["const"], 4)
                v.tensor_scalar(head_mask[:, :], head_mask[:, :], sigma[:, 0:1], DH ** -0.5 / N, ALU.mult, ALU.mult)\
                    .then_inc(S["centred"], 1)
                dve.wait_ge(S["centred"], 7)

            def fold_experts():
                dve.wait_ge(S["w_in"], 16 * 7)
                v.tensor_tensor(we, we, we_last, ALU.subtract).then_inc(S["folded"], 1)
                v.tensor_tensor(wr[:, :], wr[:, :], wr_last[:, :], ALU.subtract).then_inc(S["folded"], 1)

            def largest_experts():
                dve.wait_ge(S["w_cast"], 32)
                for k, w in ((1, we), (2, wr[:, :])):
                    v.tensor_reduce(wmax[:, k:k + 1], w, op=ALU.max, axis=AX_X, apply_absolute_value=True).then_inc(S["emaxed"], 1)

            def split_experts():
                dve.wait_ge(S["eall"], 1)
                v.tensor_scalar(wgmax[:, 1:3], wgmax[:, 1:3], 1e-30, None, ALU.max).then_inc(S["escaled"], 1)
                dve.wait_ge(S["escaled"], 1)
                v.reciprocal(wscale[:, 1:3], wgmax[:, 1:3]).then_inc(S["escaled"], 1)
                v.tensor_scalar(sigma[:, 1:3], wgmax[:, 1:3], 1.0 / (WS * XS), None, ALU.mult).then_inc(S["escaled"], 1)
                dve.wait_ge(S["escaled"], 3)
                for k, w in ((1, we), (2, wr[:, :])):
                    v.tensor_scalar(w, w, wscale[:, k:k + 1], WS, ALU.mult, ALU.mult).then_inc(S["escaled"], 1)
                dve.wait_ge(S["escaled"], 5)
                for w, hi in ((we, we_h), (wr[:, :], wr_h)):
                    v.tensor_copy(hi[:, :], w).then_inc(S["esplit"], 1)
                dve.wait_ge(S["esplit"], 2)
                for w, hi, lo in ((we, we_h, we_l), (wr[:, :], wr_h, wr_l)):
                    v.tensor_tensor(lo[:, :], w, hi[:, :], ALU.subtract).then_inc(S["esplit"], 1)

            def stats1(n, b, g, t):
                if runs(n, "st1"):
                    if t == 0:
                        at_least(dve, S["squares"], n)
                        dve.wait_ge(xa_in[g % 4], b * (BLOCK // 4 * 16) + (g // 4 + 1) * 16)
                    last = v.bn_stats(st[:, t, :], xa[:, g % 4, tile_of(t)])
                    if t == T - 1:
                        last.then_inc(S["st1"], 1)

            def stats3(n, g, t):
                if runs(n, "st3"):
                    m, r = n - LAG["st3"], (g - LAG["st3"]) % 2
                    if t == 0:
                        at_least(dve, S["o"], m + 1)
                        at_least(dve, S["squares"], n)
                    last = v.bn_stats(st[:, T + t, :], o_ps[:, tile_of(t)])
                    if t == T - 1:
                        last.then_inc(S["st3"], 1)

            def stats2(n, g, t):
                if runs(n, "st2"):
                    m, r = n - LAG["st2"], (g - LAG["st2"]) % 8
                    if t == 0:
                        at_least(dve, S["x2"], m + 1)
                        at_least(dve, S["squares"], n)
                    last = v.bn_stats(st[:, 2 * T + t, :], x2[:, r, tile_of(t)])
                    if t == T - 1:
                        last.then_inc(S["st2"], 1)

            def moments_parts(n):
                at_least(dve, S["st1"], upto(n - LAG["st1"]))
                at_least(dve, S["st3"], upto(n - LAG["st3"]))
                at_least(dve, S["st2"], upto(n - LAG["st2"]))
                at_least(dve, S["nmr"], n)
                v.tensor_tensor(sd[:, :], st[:, :, 1], st[:, :, 4], ALU.subtract)
                v.tensor_tensor(sm[:, :], st[:, :, 1], st[:, :, 4], ALU.add)
                v.scalar_tensor_tensor(out=s1[:, :], in0=st[:, :, 2], scalar=1.0 / P, in1=eps[:, :],
                                       op0=ALU.mult, op1=ALU.add).then_inc(S["sparts"], 1)

            def moments_squares(n):
                dve.wait_ge(S["sparts"], n + 1)
                at_least(dve, S["var"], n)
                v.scalar_tensor_tensor(out=sq[:, :], in0=sd[:, :], scalar=0.25, in1=sd[:, :], op0=ALU.mult, op1=ALU.mult)
                v.scalar_tensor_tensor(out=s2[:, :], in0=st[:, :, 5], scalar=1.0 / P, in1=s1[:, :],
                                       op0=ALU.mult, op1=ALU.add).then_inc(S["squares"], 1)

            def moments_var(n):
                dve.wait_ge(S["squares"], n + 1)
                at_least(dve, S["lnv"], n)
                v.tensor_tensor(var[:, :], sq[:, :], s2[:, :], ALU.add).then_inc(S["var"], 1)

            def moments_mean(n):
                at_least(dve, S["rs"], n + 1)
                at_least(dve, S["xn1"], upto(n - 1 - LAG["st1"]))
                at_least(dve, S["xn2"], upto(n - 1 - LAG["st2"]))
                at_least(dve, S["xn2p"], upto(n - 1 - LAG["st2"]))
                v.scalar_tensor_tensor(out=nmr[:, :], in0=sm[:, :], scalar=-0.5, in1=rs[:, :],
                                       op0=ALU.mult, op1=ALU.mult).then_inc(S["nmr"], 1)

            def weigh(n, g, t, e):
                if not runs(n, "weigh"):
                    return
                m, r = n - LAG["weigh"], (g - LAG["weigh"]) % 8
                if e == 0:
                    at_least(dve, S["gate"], m + 1)
                    if t == 0:
                        at_least(dve, S["x2"], m + 1)
                        at_least(dve, y_out[r % 4], stores_before(m, r))
                    at_least(dve, S["expv"], m * T + t + 1)
                else:
                    dve.wait_ge(S["acc"], m * ACC + t * HALF + e)
                a = acc[:, r % 4, tile_of(t)]
                v.scalar_tensor_tensor(out=a, in0=unit_bank(2 * t)[:, e * P:(e + 1) * P],
                                       scalar=gate[:, r % 2, t, e:e + 1],
                                       in1=x2[:, r, tile_of(t)] if e == 0 else a,
                                       op0=ALU.mult, op1=ALU.add).then_inc(S["acc"], 1)

            def split1(n, g):
                if runs(n, "lo1"):
                    at_least(dve, S["hi1"], n - LAG["lo1"] + 1)
                    v.tensor_tensor(x1l[:, :], t0[:, :], x1h[:, :], ALU.subtract).then_inc(S["lo1"], 1)

            def split2(n, g):
                if runs(n, "lo2"):
                    m, r = n - LAG["lo2"], (g - LAG["lo2"]) % 4
                    at_least(dve, S["hi2"], m + 1)
                    v.tensor_tensor(x2l[0:P - 1, r, :], t1[0:P - 1, :], x2h[0:P - 1, r, :], ALU.subtract).then_inc(S["lo2"], 1)

            def max_q(n, g):
                if runs(n, "qmax"):
                    at_least(dve, S["v"], n - LAG["qmax"] + 1)
                    at_least(dve, S["qsub"], n - LAG["qmax"])
                    v.tensor_reduce(qmax[:, :].rearrange("p (t h) -> p t h", t=T),
                                    q_ps.rearrange("p t (h k) -> p t h k", k=DH), op=ALU.max, axis=AX_X).then_inc(S["qmax"], 1)

            def subtract_qmax(n, g):
                if runs(n, "qsub"):
                    m, r = n - LAG["qsub"], (g - LAG["qsub"]) % BLOCK
                    dve.wait_ge(S["qmax"], m + 1)
                    at_least(dve, S["qn"], m - BLOCK + 1)
                    v.tensor_tensor(qe[:, r, :].rearrange("p (t h k) -> p t h k", t=T, k=DH),
                                    q_ps.rearrange("p t (h k) -> p t h k", k=DH),
                                    qmax[:, :].rearrange("p (t h) -> p t h", t=T).unsqueeze(3).to_broadcast([P, T, HEADS, DH]),
                                    ALU.subtract).then_inc(S["qsub"], 1)

            def max_k(n, g):
                if runs(n, "kmax"):
                    m = n - LAG["kmax"]
                    at_least(dve, S["kt"], m + 1)
                    at_least(dve, S["bound"], m)
                    v.tensor_reduce(kmax[:, :], pk[:, :], op=ALU.max, axis=AX_X).then_inc(S["kmax"], 1)

            def bound_k(n, g):
                if runs(n, "nk"):
                    m, r = n - LAG["nk"], (g - LAG["nk"]) % G
                    dve.wait_ge(S["kmax"], m + 1)
                    at_least(dve, S["kexp"], m - 1)
                    at_least(dve, S["shrink"], m)
                    new, old = bound[:, r % 2:r % 2 + 1], bound[:, (r - 1) % 2:(r - 1) % 2 + 1]
                    if r == 0:
                        v.tensor_scalar(new, kmax[:, :], sigma[:, 3:4], None, ALU.mult).then_inc(S["bound"], 1)
                    else:
                        v.scalar_tensor_tensor(out=new, in0=kmax[:, :], scalar=sigma[:, 3:4], in1=old,
                                               op0=ALU.mult, op1=ALU.min).then_inc(S["bound"], 1)

            def sum_q(n, g):
                if runs(n, "qsum"):
                    m, r = n - LAG["qsum"], (g - LAG["qsum"]) % BLOCK
                    at_least(dve, S["qexp"], m + 1)
                    at_least(dve, S["qr"], m)
                    v.tensor_reduce(qsum[:, :], qe[:, r, :].rearrange("p (h k) -> p h k", k=DH), op=ALU.add, axis=AX_X)\
                        .then_inc(S["qsum"], 1)

            def invert_qsum(n, g):
                if runs(n, "qr"):
                    m, r = n - LAG["qr"], (g - LAG["qr"]) % BLOCK
                    dve.wait_ge(S["qsum"], m + 1)
                    v.reciprocal(qr[:, r, :], qsum[:, :]).then_inc(S["qr"], 1)

            def sum_context(n, b, g):
                if runs(n, "csum"):
                    m, r = n - LAG["csum"], (g - LAG["csum"]) % G
                    at_least(dve, S["ctx"], m + 1)
                    if r == 0:
                        at_least(dve, S["cn"], batch_start(n, b, g, LAG["csum"]))
                        v.tensor_copy(csum[:, :], ctx_ps).then_inc(S["csum"], 1)
                    else:
                        dve.wait_ge(S["csum"], m)
                        dve.wait_ge(S["shrink"], m + 1)
                        v.scalar_tensor_tensor(out=csum[:, :], in0=csum[:, :], scalar=shrink[:, r % 2:r % 2 + 1], in1=ctx_ps,
                                               op0=ALU.mult, op1=ALU.add).then_inc(S["csum"], 1)

            def invert_ksum(n, b, g):
                done = batch_end(n, b, g, LAG["rk"])
                if done is not None:
                    dve.wait_ge(S["csum"], done * G)
                    v.reciprocal(rksum[:, :], csum[:, P:P + 1]).then_inc(S["rk"], 1)

            def normalise_context(n, b, g):
                done = batch_end(n, b, g, LAG["cn"])
                if done is not None:
                    dve.wait_ge(S["rk"], done)
                    at_least(dve, S["cturn"], done - 1)
                    v.scalar_tensor_tensor(out=cn[:, :], in0=csum[:, 0:P], scalar=rksum[:, 0:1], in1=head_mask[:, :],
                                           op0=ALU.mult, op1=ALU.mult).then_inc(S["cn"], 1)

            def finish_mix(n, b, g):
                done = batch_end(n, b, g, LAG["mix"])
                if done is not None:
                    dve.wait_ge(S["mixp"], done)
                    at_least(dve, S["o"], (done - 1) * G)
                    v.tensor_tensor(mix[:, :], t0[:, 0:2 * P], bo[:, :], ALU.add).then_inc(S["mix"], 1)

            def gates_logit(n, g):
                if runs(n, "logit"):
                    m = n - LAG["logit"]
                    at_least(dve, S["rout"], m + 1)
                    at_least(dve, S["topi"], m)
                    v.tensor_copy(logit[:, :, :], t1[:, 0:T * E].rearrange("p (t e) -> p t e", t=T)).then_inc(S["logit"], 1)

            def gates_top(n, g):
                if runs(n, "top"):
                    dve.wait_ge(S["logit"], n - LAG["top"] + 1)
                    step_on(dve, S["dve_go"])
                    for t in range(T):
                        last = v.max(top[:, t, :], logit[:, t, :])
                    last.then_inc(S["top"], 1)

            def gates_gap(n, g):
                if runs(n, "topi"):
                    m = n - LAG["topi"]
                    dve.wait_ge(S["top"], m + 1)
                    at_least(dve, S["e2"], m)
                    at_least(dve, S["oh1"], m)
                    at_least(dve, S["oh2"], m)
                    v.tensor_tensor(gap[:, :], top[:, :, 1], top[:, :, 0], ALU.subtract).then_inc(S["gap"], 1)
                    for t in range(T):
                        last = v.max_index(top_i[:, t, :], top[:, t, :], logit[:, t, :])
                    last.then_inc(S["topi"], 1)

            def gates_onehot(n, g, k):
                oh, step = ((oh1, "oh1"), (oh2, "oh2"))[k]
                if runs(n, step):
                    m = n - LAG[step]
                    dve.wait_ge(S["topi"], m + 1)
                    at_least(dve, S["gate"], m)
                    v.tensor_tensor(oh, expert_no[:, :, :],
                                           top_i[:, :, k:k + 1].to_broadcast([P, T, E]), ALU.is_equal).then_inc(S[step], 1)

            def gates_sum(n, g):
                if runs(n, "e2p"):
                    at_least(dve, S["e2"], n - LAG["e2p"] + 1)
                    at_least(dve, S["r2"], n - LAG["e2p"])
                    v.tensor_scalar(e2p[:, :], e2[:, :], 1.0, None, ALU.add).then_inc(S["e2p"], 1)

            def gates_recip(n, g):
                if runs(n, "r2"):
                    dve.wait_ge(S["e2p"], n - LAG["r2"] + 1)
                    at_least(dve, S["g1"], n - LAG["r2"])
                    v.reciprocal(r2[:, :], e2p[:, :]).then_inc(S["r2"], 1)

            def gates_first(n, g):
                if runs(n, "g1"):
                    m = n - LAG["g1"]
                    dve.wait_ge(S["r2"], m + 1)
                    at_least(dve, S["gb"], m)
                    at_least(dve, S["g2"], m)
                    v.tensor_scalar(g1, r2[:, :], sigma[:, 1:2], None, ALU.mult).then_inc(S["g1"], 1)

            def gates_second(n, g):
                if runs(n, "g2"):
                    m = n - LAG["g2"]
                    dve.wait_ge(S["g1"], m + 1)
                    at_least(dve, S["gb"], m)
                    v.tensor_tensor(g2, g1, e2[:, :], ALU.mult).then_inc(S["g2"], 1)

            def slot(n, b, g):
                if isinstance(n, int):
                    if n == PREPARE["fold"]:
                        fold_experts()
                        centre_w_out()
                    if n == PREPARE["largest"]:
                        largest_experts()
                    if n == PREPARE["split"]:
                        split_experts()
                stats1(n, b, g, 0)
                stats1(n, b, g, 1)
                finish_mix(n, b, g)
                max_q(n, g)
                weigh(n, g, 0, 0)
                subtract_qmax(n, g)
                weigh(n, g, 0, 1)
                stats2(n, g, 0)
                weigh(n, g, 0, 2)
                split1(n, g)
                stats1(n, b, g, 2)
                weigh(n, g, 0, 3)
                stats1(n, b, g, 3)
                stats2(n, g, 1)
                weigh(n, g, 1, 0)
                stats2(n, g, 2)
                stats2(n, g, 3)
                gates_sum(n, g)
                stats3(n, g, 0)
                stats3(n, g, 1)
                stats3(n, g, 2)
                stats3(n, g, 3)
                gates_recip(n, g)
                moments_parts(n)
                weigh(n, g, 1, 1)
                moments_squares(n)
                weigh(n, g, 1, 2)
                moments_var(n)
                gates_onehot(n, g, 1)
                weigh(n, g, 1, 3)
                gates_onehot(n, g, 0)
                weigh(n, g, 2, 0)
                gates_first(n, g)
                weigh(n, g, 2, 1)
                gates_second(n, g)
                sum_context(n, b, g)
                moments_mean(n)
                invert_ksum(n, b, g)
                split2(n, g)
                normalise_context(n, b, g)
                weigh(n, g, 2, 2)
                invert_qsum(n, g)
                max_k(n, g)
                gates_logit(n, g)
                weigh(n, g, 2, 3)
                gates_top(n, g)
                bound_k(n, g)
                sum_q(n, g)
                gates_gap(n, g)

            all_slots(dve, slot)


_INS = ["x", "L0_conv_w_qkv", "L0_conv_w_out", "L0_conv_b_out", "L0_conv_ln_scale",
        "L0_ffn_router_w", "L0_ffn_router_b", "L0_ffn_expert_w", "L0_ffn_expert_b"]


def kernel(**inputs):
    import numpy as _np
    import concourse.bacc as _bacc
    from concourse import mybir as _mybir
    from concourse.bass_utils import run_bass_kernel_spmd as _run

    nc = _bacc.Bacc("TRN2", target_bir_lowering=False, num_devices=1)
    arrays, args = {}, []
    for name in _INS:
        a = _np.ascontiguousarray(inputs[name])
        arrays[f"in_{name}"] = a
        args.append(nc.dram_tensor(f"in_{name}", a.shape, _mybir.dt.from_np(a.dtype), kind="ExternalInput").ap())
    args.append(nc.dram_tensor("out_0", inputs["x"].shape, F32, kind="ExternalOutput").ap())
    metaformer_kernel(nc, *args)
    r = _run(nc, [arrays], core_ids=[0])
    return r.results[0]["out_0"]
```
